# Optimizing a Trainium2 kernel written in Bass

```python
import numpy as np
import jax
import jax.numpy as jnp

def _softmax(x, axis=-1):
    return jax.nn.softmax(x, axis=axis)

def _gelu(x):
    return jax.nn.gelu(x, approximate=True)

def _silu(x):
    return jax.nn.silu(x)

def _sigmoid(x):
    return jax.nn.sigmoid(x)

def _layernorm(x, axis=-1, eps=1e-05):
    m = jnp.mean(x, axis=axis, keepdims=True)
    v = jnp.var(x, axis=axis, keepdims=True)
    return (x - m) / jnp.sqrt(v + eps)

def _scatter_add(tgt, idx, src, axis=0):
    return tgt.at[idx].add(src)

def _segment_sum(src, seg, n):
    return jax.ops.segment_sum(src, seg, n)
kernel_name = 'mk_adaln_attn_ffn_d1_seqx_r8_74b6df'

def setup_inputs(seed: int=0):
    np.random.seed(seed)
    _w = jnp.asarray

    def _rec_inputs():
        import jax
        import jax.numpy as jnp
        _rk = jax.random.key(seed)
        x = -0.000125 + 0.9999 * jax.random.normal(jax.random.fold_in(_rk, 1), (8, 128, 512), jnp.float32)
        _lenS = 128 - jax.random.randint(jax.random.fold_in(_rk, 7), (8,), 0, max(1, 128 // 4) + 1, jnp.int32)
        _lenS2 = 128 - jax.random.randint(jax.random.fold_in(_rk, 8), (8,), 0, max(1, 128 // 4) + 1, jnp.int32)
        itok_B_14_62 = jax.random.randint(jax.random.fold_in(_rk, 11), (8,), 14, 63, jnp.int32)
        itok_B_3_7 = jax.random.randint(jax.random.fold_in(_rk, 12), (8,), 3, 8, jnp.int32)
        return (x, itok_B_14_62, itok_B_3_7)
    x, itok_B_14_62, itok_B_3_7 = _rec_inputs()

    def _L0_cond_setup():
        import jax, jax.numpy as jnp
        import numpy as np
        B, S, D_IN, D_OUT = (4, 256, 512, 512)
        L, R = (64, 16)
        LORA_ALPHA = 32
        LORA_SCALING = LORA_ALPHA / R
        key = jax.random.key(seed)
        k = jax.random.split(key, 6)
        return {'X': jax.random.normal(k[0], (B, S, D_IN), dtype=jnp.float32), 'W': jax.random.normal(k[1], (D_OUT, D_IN), dtype=jnp.float32) * (1.0 / np.sqrt(D_IN)), 'b': jax.random.normal(k[2], (D_OUT,), dtype=jnp.float32), 'lora_A': jax.random.normal(k[3], (L, D_IN, R), dtype=jnp.float32) * (1.0 / np.sqrt(D_IN)), 'lora_B': jax.random.normal(k[4], (L, D_OUT, R), dtype=jnp.float32) * (1.0 / np.sqrt(D_OUT)), 'lora_ids': jax.random.randint(k[5], (B,), 0, L, dtype=jnp.int64)}
    _L0_cond_all = _L0_cond_setup()
    _L0_cond_in = {k: v for k, v in _L0_cond_all.items() if k in ('W', 'b', 'lora_A', 'lora_B')}
    del _L0_cond_all

    def _L0_attn_setup():
        import jax, jax.numpy as jnp
        import numpy as np
        B, T, D = (1, 256, 512)
        H, G = (32, 8)
        HD = D // H
        REP = H // G
        KV_DIM = 2 * HD * G
        key = jax.random.key(seed)
        k0, k1, k2, k3 = jax.random.split(key, 4)
        x = jax.random.normal(k0, (B, T, D), dtype=jnp.float32)
        Wq = jax.random.normal(k1, (D, D), dtype=jnp.float32) * 0.02
        Wkv = jax.random.normal(k2, (D, KV_DIM), dtype=jnp.float32) * 0.02
        Wo = jax.random.normal(k3, (D, D), dtype=jnp.float32) * 0.02
        bo = jnp.zeros((D,), dtype=jnp.float32)
        return {'x': x, 'Wq': Wq, 'Wkv': Wkv, 'Wo': Wo, 'bo': bo}
    _L0_attn_all = _L0_attn_setup()
    _L0_attn_in = {k: v for k, v in _L0_attn_all.items() if k in ('Wq', 'Wkv', 'Wo', 'bo')}
    del _L0_attn_all

    def _L0_cond2_setup():
        import jax, jax.numpy as jnp
        import numpy as np
        RANK = 16
        ALPHA = 16.0
        SCALING = ALPHA / RANK
        N_ADAPTERS = 8
        IN_F = 512
        OUT_F = 512
        BATCH = 4
        SEQ = 256
        key = jax.random.key(seed)
        kx, ka, kb, ki = jax.random.split(key, 4)
        x = jax.random.normal(kx, (BATCH, SEQ, IN_F), dtype=jnp.float32)
        A = jax.random.normal(ka, (N_ADAPTERS, OUT_F, RANK), dtype=jnp.float32) * 0.02
        B = jax.random.normal(kb, (N_ADAPTERS, RANK, IN_F), dtype=jnp.float32) * 0.02
        adapter_ids = jax.random.randint(ki, (BATCH,), 0, N_ADAPTERS, dtype=jnp.int32)
        return {'x': x, 'A': A, 'B': B, 'adapter_ids': adapter_ids}
    _L0_cond2_all = _L0_cond2_setup()
    _L0_cond2_in = {k: v for k, v in _L0_cond2_all.items() if k in ('A', 'B')}
    del _L0_cond2_all

    def _L0_ffn_setup():
        import jax, jax.numpy as jnp
        import numpy as np
        BATCH, SEQ, D = (2, 256, 512)
        K, TOPK, RANK = (64, 16, 16)
        ALPHA = 32.0
        SCALING = ALPHA / RANK
        key = jax.random.key(seed)
        k1, k2, k3, k4 = jax.random.split(key, 4)
        x = jax.random.normal(k1, (BATCH, SEQ, D), dtype=jnp.float32)
        A = jax.random.normal(k2, (K, RANK, D), dtype=jnp.float32) * 0.02
        B = jax.random.normal(k3, (K, D, RANK), dtype=jnp.float32) * 0.02
        Wr = jax.random.normal(k4, (K, D), dtype=jnp.float32) * 0.02
        return {'x': x, 'A': A, 'B': B, 'Wr': Wr}
    _L0_ffn_all = _L0_ffn_setup()
    _L0_ffn_in = {k: v for k, v in _L0_ffn_all.items() if k in ('A', 'B', 'Wr')}
    del _L0_ffn_all
    return {'x': x, 'itok_B_14_62': itok_B_14_62, 'itok_B_3_7': itok_B_3_7, 'L0_cond_W': _L0_cond_in['W'], 'L0_cond_b': _L0_cond_in['b'], 'L0_cond_lora_A': _L0_cond_in['lora_A'], 'L0_cond_lora_B': _L0_cond_in['lora_B'], 'L0_attn_Wq': _L0_attn_in['Wq'], 'L0_attn_Wkv': _L0_attn_in['Wkv'], 'L0_attn_Wo': _L0_attn_in['Wo'], 'L0_attn_bo': _L0_attn_in['bo'], 'L0_cond2_A': _L0_cond2_in['A'], 'L0_cond2_B': _L0_cond2_in['B'], 'L0_ffn_A': _L0_ffn_in['A'], 'L0_ffn_B': _L0_ffn_in['B'], 'L0_ffn_Wr': _L0_ffn_in['Wr']}

def reference(x, itok_B_14_62, itok_B_3_7, L0_cond_W, L0_cond_b, L0_cond_lora_A, L0_cond_lora_B, L0_attn_Wq, L0_attn_Wkv, L0_attn_Wo, L0_attn_bo, L0_cond2_A, L0_cond2_B, L0_ffn_A, L0_ffn_B, L0_ffn_Wr):
    import jax
    import jax.numpy as jnp

    def _L0_cond_ref(X, W, b, lora_A, lora_B, lora_ids):
        import jax, jax.numpy as jnp
        import numpy as np
        B, S, D_IN, D_OUT = (4, 256, 512, 512)
        L, R = (64, 16)
        LORA_ALPHA = 32
        LORA_SCALING = LORA_ALPHA / R
        output = jnp.einsum('bsd,od->bso', X, W) + b
        A = lora_A[lora_ids]
        Bm = lora_B[lora_ids]
        inter = jnp.einsum('bwr,bsw->bsr', A, X)
        lora_out = output + jnp.einsum('bsr,bwr->bsw', inter, Bm) * LORA_SCALING
        return lora_out

    def _L0_attn_ref(x, Wq, Wkv, Wo, bo):
        import jax, jax.numpy as jnp
        import numpy as np
        B, T, D = (1, 256, 512)
        H, G = (32, 8)
        HD = D // H
        REP = H // G
        KV_DIM = 2 * HD * G
        b, t, d = x.shape
        q = jnp.dot(x, Wq).reshape(b, t, H, HD).transpose(0, 2, 1, 3)
        kv = jnp.dot(x, Wkv).reshape(b, t, G, 2, HD).transpose(2, 3, 0, 1, 4)
        k, v = (kv[:, 0], kv[:, 1])
        k = jnp.broadcast_to(k[:, :, None], (G, b, REP, t, HD)).reshape(b, H, t, HD)
        v = jnp.broadcast_to(v[:, :, None], (G, b, REP, t, HD)).reshape(b, H, t, HD)
        scores = jnp.einsum('bhqd,bhkd->bhqk', q, k)
        causal = jnp.triu(jnp.ones((t, t), dtype=bool), 1)
        scores = jnp.where(causal[None, None], -jnp.inf, scores)
        weights = jax.nn.softmax(scores * (1.0 / HD ** 0.5), axis=-1)
        ctx = jnp.einsum('bhqk,bhkd->bhqd', weights, v)
        ctx = ctx.transpose(0, 2, 1, 3).reshape(b, t, d)
        return jnp.dot(ctx, Wo) + bo

    def _L0_cond2_ref(x, A, B, adapter_ids):
        import jax, jax.numpy as jnp
        import numpy as np
        RANK = 16
        ALPHA = 16.0
        SCALING = ALPHA / RANK
        N_ADAPTERS = 8
        IN_F = 512
        OUT_F = 512
        BATCH = 4
        SEQ = 256
        B_sel = B[adapter_ids]
        A_sel = A[adapter_ids]
        Bx = jnp.einsum('bni,bri->bnr', x, B_sel)
        out = jnp.einsum('bnr,bor->bno', Bx, A_sel)
        return out * SCALING

    def _L0_ffn_ref(x, A, B, Wr):
        import jax, jax.numpy as jnp
        import numpy as np
        BATCH, SEQ, D = (2, 256, 512)
        K, TOPK, RANK = (64, 16, 16)
        ALPHA = 32.0
        SCALING = ALPHA / RANK
        prefix = x.shape[:-1]
        xf = x.reshape(-1, x.shape[-1])
        N = xf.shape[0]
        scores = xf @ Wr.T
        top_vals, top_idx = jax.lax.top_k(scores, TOPK)
        gates = jax.nn.softmax(top_vals, axis=-1)
        G = jnp.zeros((N, K), xf.dtype).at[jnp.arange(N)[:, None], top_idx].set(gates)
        h = jnp.einsum('nd,krd->nkr', xf, A)
        out = jnp.einsum('nkr,kdr->nd', h * G[:, :, None], B)
        return (out * SCALING).reshape(*prefix, -1)
    x = x + _L0_attn_ref(_L0_cond_ref(x, L0_cond_W, L0_cond_b, L0_cond_lora_A, L0_cond_lora_B, itok_B_14_62), L0_attn_Wq, L0_attn_Wkv, L0_attn_Wo, L0_attn_bo)
    x = x + _L0_ffn_ref(_L0_cond2_ref(x, L0_cond2_A, L0_cond2_B, itok_B_3_7), L0_ffn_A, L0_ffn_B, L0_ffn_Wr)
    return x

_drawn_inputs = setup_inputs


def setup_inputs(seed=0):
    import zlib

    import numpy as np

    out = dict(_drawn_inputs(seed))
    spreads = {'L0_attn_bo': (0.0, 0.1)}
    factors = {'L0_cond_lora_A': 3.103,
     'L0_cond_lora_B': 3.021,
     'L0_cond2_A': 8.0,
     'L0_cond2_B': 8.0,
     'L0_ffn_A': 8.0,
     'L0_ffn_B': 8.0,
     'L0_ffn_Wr': 8.0}
    for name, (base, spread) in spreads.items():
        noise = np.random.default_rng([zlib.crc32(name.encode()), seed]).standard_normal(out[name].shape)
        drawn = base * np.exp(spread * noise) if base else spread * noise
        out[name] = jnp.asarray(drawn.astype(out[name].dtype))
    for name, factor in factors.items():
        out[name] = (out[name] * factor).astype(out[name].dtype)
    return out
```

```python
from contextlib import ExitStack

import concourse.bass as bass
from concourse import mybir

F32 = mybir.dt.float32
BF16 = mybir.dt.bfloat16
I32 = mybir.dt.int32
ALU = mybir.AluOpType
ACT = mybir.ActivationFunctionType
AX_X = mybir.AxisListType.X

P = 128


def adaln_attn_ffn_kernel(nc, x, cond_ids, cond2_ids, W, b, lora_A, lora_B, Wq, Wkv, Wo, bo,
                          cond2_A, cond2_B, ffn_A, ffn_B, Wr, out):
    NBATCH, T, D = x.shape
    NPAIR = NBATCH // 2
    R = lora_A.shape[2]
    NLORA, NCOND2 = lora_A.shape[0], cond2_A.shape[0]
    KV = Wkv.shape[1]
    H, G, HD = 32, 8, 16
    REP = H // G
    C = D // P
    K, RF, _ = ffn_A.shape
    NI = K * RF // P
    NH = K * RF
    TOP8 = 2
    SCALE = float(HD) ** -0.5
    LORA_SCALE, FFN_SCALE = 2.0, 2.0
    FAR = -3.0e38
    assert T == P and NBATCH * R == P and G * HD == P and C == REP == 4 and 2 * K == P

    with ExitStack() as ctx:
        def sb(name, shape, dt=F32):
            return ctx.enter_context(nc.sbuf_tensor(name, shape, dt))

        def sem(name):
            return ctx.enter_context(nc.semaphore(name))

        def sems(name):
            return [sem(f"{name}{s}") for s in range(2)]

        ident = sb("ident", [P, P])
        identb = sb("identb", [P, P], BF16)
        causal = sb("causal", [P, 4, P], BF16)
        own = sb("own", [P, NBATCH])
        own2 = sb("own2", [P, NBATCH])
        maxsel = sb("maxsel", [P, G, P], BF16)
        onespad = sb("onespad", [P, 2, 32])
        w_sb = sb("w_sb", [P, C, D])
        wq_sb = sb("wq_sb", [P, C, D])
        wkv_sb = sb("wkv_sb", [P, C, KV])
        wo_sb = sb("wo_sb", [P, REP, D])
        b_sb = sb("b_sb", [P, C])
        bo_sb = sb("bo_sb", [P, C])
        bo_bc = sb("bo_bc", [P, D])
        ids = sb("ids", [1, 2, NBATCH], I32)
        la_sb = sb("la_sb", [P, C, NBATCH * R])
        lb_sb = sb("lb_sb", [P, C, NBATCH * R])
        ca_sb = sb("ca_sb", [P, C, NBATCH * R])
        cb_sb = sb("cb_sb", [P, D])
        fa_sb = sb("fa_sb", [P, NI, D])
        PT_fb = sb("PT_fb", [P, 2 * G * 4 * P])
        fb_raw = PT_fb[:, 0:D * RF]
        wr_sb = sb("wr_sb", [K, D])
        wf = sb("wf", [P, C + 2, D + KV])
        bq = sb("bq", [P, REP])
        bkv_bc = wf[:, C + 1, D:D + KV]
        cbT = sb("cbT", [P, C, P])
        woT = sb("woT", [P, C, REP, P])
        wob = sb("wob", [P, REP, P])
        bz = sb("bz", [P, 1])
        faT = sb("faT", [P, C, NH + K])
        mm = sb("mm", [P, NH + K])
        fb_sb = sb("fb_sb", [P, NI, D])
        xs = [sb(f"xs{s}", [P, D]) for s in range(2)]
        xr = [sb(f"xr{s}", [P, D]) for s in range(2)]
        xT = sb("xT", [P, C, 2, P])
        uT = sb("uT", [P, 2, P])
        qT_all = fa_sb[:, :, :].rearrange("p n (r t) -> p n r t", r=REP)
        kn = woT[:, 0:2].rearrange("p a r n -> p (a r n)").rearrange("p (g j d) -> p g j d", g=G, j=G)
        vn = woT[:, 2:4].rearrange("p a r n -> p (a r n)").rearrange("p (g j d) -> p g j d", g=G, j=G)
        zx = wkv_sb[:, :, :].rearrange("p c n -> p (c n)").rearrange("p (n t) -> p n t", n=NBATCH)
        kT_all = sb("kT_all", [P, G, P])
        kTm = [sb(f"kTm{s}", [P, G, P]) for s in range(2)]
        vpad = [sb(f"vpad{s}", [P, G, 32]) for s in range(2)]
        qT = [sb(f"qT{s}", [P, REP, P]) for s in range(2)]
        mx = [sb(f"mx{s}", [P, REP, G]) for s in range(2)]
        mhl = [sb(f"mhl{s}", [P, REP, G, 2], BF16) for s in range(2)]
        mT = [sb(f"mT{s}", [P, 4 * P], BF16) for s in range(2)]
        PT = [PT_fb[:, s * G * 4 * P:(s + 1) * G * 4 * P].rearrange("p (g n) -> p g n", g=G) for s in range(2)]
        rden = sb("rden", [P, 4 * P])
        ctxT = sb("ctxT", [P, REP, 2, P])
        zT = [sb(f"zT{s}", [P, P]) for s in range(2)]
        rs = [sb(f"rs{s}", [P, K]) for s in range(2)]
        rest = [sb(f"rest{s}", [P, K]) for s in range(2)]
        top = [sb(f"top{s}", [P, 8 * TOP8]) for s in range(2)]
        nmax = [sb(f"nmax{s}", [P, 1]) for s in range(2)]
        ex = [sb(f"ex{s}", [P, K]) for s in range(2)]
        gate = [sb(f"gate{s}", [P, K]) for s in range(2)]
        gsum = [sb(f"gsum{s}", [P, 2]) for s in range(2)]
        faT_flat = faT[:, :, :].rearrange("p c n -> p (c n)")
        hG = [faT_flat[:, s * NH:(s + 1) * NH] for s in range(2)]
        hGT = [faT_flat[:, (2 + s) * NH:(3 + s) * NH].rearrange("p (i t) -> p i t", i=NI) for s in range(2)]
        fin = [sb(f"fin{s}", [P, D]) for s in range(2)]

        X = [ctx.enter_context(nc.psum_tensor(f"X{s}", [P, 1024], F32)) for s in range(2)]
        CX = [ctx.enter_context(nc.psum_tensor(f"CX{s}", [P, 512], F32)) for s in range(2)]
        DN = [ctx.enter_context(nc.psum_tensor(f"DN{s}", [P, 512], F32)) for s in range(2)]
        bank = [X[0][:, 0:512], X[0][:, 512:1024], X[1][:, 0:512], X[1][:, 512:1024],
                CX[0][:, :], CX[1][:, :], DN[0][:, :], DN[1][:, :]]
        NB = len(bank)

        consts = sem("consts")
        pool_step = sem("pool_step")
        zeroed = sem("zeroed")
        dve_passed, pool_passed = sem("dve_passed"), sem("pool_passed")
        ids_in = sem("ids_in")
        w_in = sem("w_in")
        bias_in = sem("bias_in")
        lora_in = sem("lora_in")
        cond2_in = sem("cond2_in")
        wo_in = sem("wo_in")
        fa_in = sem("fa_in")
        fb_in = sem("fb_in")
        fb_ready = sem("fb_ready")
        pre_ps = sem("pre_ps")
        pre_out = [sem("pre_dve"), sem("pre_act")]
        x_in = sems("x_in")
        xr_in = sems("xr_in")
        xT_ps, xT_ready = sem("xT_ps"), sem("xT_ready")
        u_ps, u_ready = sem("u_ps"), sem("u_ready")
        kv_ps, kv_ready, zx_ps, zx_ready = sem("kv_ps"), sem("kv_ready"), sem("zx_ps"), sem("zx_ready")
        kT_ps, kT_ready, operands = sem("kT_ps"), sem("kT_ready"), sems("operands")
        q_ps, q_ready = sem("q_ps"), sem("q_ready")
        s_ps, max_ready, mhi_ready, m_ready = sems("s_ps"), sems("max_ready"), sems("mhi_ready"), sems("m_ready")
        mT_ps, mT_ready = sems("mT_ps"), sems("mT_ready")
        st_ps, exp_ready, pm_ready = sems("st_ps"), sems("exp_ready"), sems("pm_ready")
        pv_ps, rden_ready, ctx_ready = sems("pv_ps"), sems("rden_ready"), sems("ctx_ready")
        z_ps, z_ready = sem("z_ps"), sems("z_ready")
        r_ps, h_ps = sems("r_ps"), sems("h_ps")
        topk, gexp = sems("topk"), sems("gexp")
        hG_ready, hGT_ps, hGT_ready = sems("hG_ready"), sems("hGT_ps"), sems("hGT_ready")
        o_ps, xb_ready, fin_ready, stored = sems("o_ps"), sems("xb_ready"), sems("fin_ready"), sems("stored")

        fold = [("fold", c, part) for c in range(C + 2) for part in ("q", "kv")]
        jobs = fold + [("bias_cols", 0, ""), ("cbT", 0, "")]
        jobs += [("woT", r, "") for r in range(REP)] + [("faT", i, "") for i in range(NI)] + [("wrT", 0, "")]
        jobs += [("wob", 0, ""), ("bz", 0, "")] + [("mm", n, "") for n in range(3)]
        at = {job[:2] if job[0] != "fold" else job: j for j, job in enumerate(jobs)}

        def job_io(job):
            kind, n, part = job
            o = bank[at[job if kind == "fold" else job[:2]] % NB]
            if kind == "fold" and part == "q":
                return (o.rearrange("p (g r d) -> p r g d", g=G, r=REP),
                        wf[:, n, 0:D].rearrange("p (r g d) -> p r g d", r=REP, g=G))
            if kind == "fold":
                return (o[:, 0:KV].rearrange("p (g t d) -> p t g d", g=G, t=2),
                        wf[:, n, D:D + KV].rearrange("p (t g d) -> p t g d", t=2, g=G))
            if kind == "bias_cols":
                return o[:, 0:REP], bq[:, :]
            if kind == "cbT":
                return o.rearrange("p (c n) -> p c n", c=C), cbT[:, :, :]
            if kind == "woT":
                return o.rearrange("p (c n) -> p c n", c=C), woT[:, :, n, :]
            if kind == "faT":
                return o.rearrange("p (c n) -> p c n", c=C), faT[:, :, n * P:(n + 1) * P]
            if kind == "wrT":
                return o[:, 0:C * K].rearrange("p (c n) -> p c n", c=C), faT[:, :, NH:NH + K]
            if kind == "wob":
                return o.rearrange("p (r n) -> p r n", r=REP), wob[:, :, :]
            if kind == "bz":
                return o[:, 0:1], bz[:, :]
            lo, hi = 512 * n, min(512 * n + 512, NH + K)
            return o[:, 0:hi - lo], mm[:, lo:hi]

        def wait_jobs(eng, n):
            eng.wait_ge(pre_out[0], (n + 1) // 2)
            eng.wait_ge(pre_out[1], n // 2)

        block = ctx.enter_context(nc.Block())

        @block.sync
        def _(sp):
            sp.dma_start(ids[:, 0, :], cond_ids.rearrange("(a n) -> a n", a=1)).then_inc(ids_in, 16)
            sp.dma_start(ids[:, 1, :], cond2_ids.rearrange("(a n) -> a n", a=1)).then_inc(ids_in, 16)
            sp.dma_start(w_sb[:, :, :], W.rearrange("(p c) n -> p c n", c=C)).then_inc(w_in, 16)
            for s in range(2):
                sp.dma_start(xs[s][:, :], x[s]).then_inc(x_in[s], 16)
            sp.wait_ge(ids_in, 32)
            with sp.Fori(0, NBATCH) as n:
                a = sp.value_load(ids[0:1, 0, bass.ds(n, 1)], min_val=0, max_val=NLORA - 1)
                sp.dma_start(lb_sb[:, :, bass.ds(R * n, R)], lora_B[bass.ds(a, 1)].rearrange(
                    "a (p c) r -> p (a c) r", c=C)).then_inc(lora_in, 16)
                sp.dma_start(la_sb[:, :, bass.ds(R * n, R)], lora_A[bass.ds(a, 1)].rearrange(
                    "a (p c) r -> p (a c) r", c=C)).then_inc(lora_in, 16)
            sp.dma_start(wr_sb[:, :], Wr).then_inc(fa_in, 16)
            for c2 in range(2):
                sp.dma_start(fa_sb[K * c2:K * (c2 + 1), :, :],
                             ffn_A.rearrange("k (i c) n -> c k i n", c=2)[c2]).then_inc(fa_in, 16)
            fbv = ffn_B.rearrange("k n r -> k (n r)")
            sp.dma_start(fb_raw[0:K, :], fbv).then_inc(fb_in, 16)
            sp.dma_start(fb_raw[K:2 * K, 0:D * RF - 1], fbv[:, 1:D * RF]).then_inc(fb_in, 16)
            with sp.Fori(0, NPAIR - 1) as i:
                sp.wait_ge(xT_ps, 2 * i + 2)
                for s in range(2):
                    sp.dma_start(xs[s][:, :], x[bass.ds(2 * i + 2 + s, 1)].rearrange("a t n -> (a t) n"))\
                      .then_inc(x_in[s], 16)
            for s in range(2):
                sp.dma_start(xr[s][:, :], x[s]).then_inc(xr_in[s], 16)

            def store(i, s):
                sp.wait_ge(fin_ready[s], i + 1)
                sp.dma_start(out[bass.ds(2 * i + s, 1)].rearrange("a t n -> (a t) n"), fin[s][:, :])\
                  .then_inc(stored[s], 16)

            with sp.Fori(0, NPAIR - 1) as i:
                for s in range(2):
                    store(i, s)
                    sp.dma_start(xr[s][:, :], x[bass.ds(2 * i + 2 + s, 1)].rearrange("a t n -> (a t) n"))\
                      .then_inc(xr_in[s], 16)
            for s in range(2):
                store(NPAIR - 1, s)
            for s in range(2):
                sp.wait_ge(stored[s], 16 * NPAIR)

        @block.gpsimd
        def _(pool):
            steps = [0]

            def then_wait(ins):
                steps[0] += 1
                ins.then_inc(pool_step, 1)
                pool.wait_ge(pool_step, steps[0])

            def band(t, low, high, pattern):
                then_wait(pool.memset(t, 1.0))
                then_wait(pool.affine_select(out=t, in_=t, compare_op=ALU.is_ge, fill=0.0, base=-low,
                                             pattern=[[-a, n] for a, n in pattern], channel_multiplier=1))
                then_wait(pool.affine_select(out=t, in_=t, compare_op=ALU.is_ge, fill=0.0, base=high,
                                             pattern=[[a, n] for a, n in pattern], channel_multiplier=-1))

            band(ident[:, :], 0, 0, [(1, P)])
            then_wait(pool.tensor_copy(identb[:, :], ident[:, :]))
            band(own[:, :], 0, R - 1, [(R, NBATCH)])
            then_wait(pool.tensor_scalar(own2[:, :], own[:, :], LORA_SCALE, None, ALU.mult))
            then_wait(pool.memset(causal[:, :, :], 0.0))
            then_wait(pool.affine_select(out=causal[:, :, :], in_=causal[:, :, :], compare_op=ALU.is_ge,
                                         fill=FAR, base=0, pattern=[[0, 4], [-1, P]], channel_multiplier=1))
            band(maxsel[:, :, :], 0, 1, [(2, G), (0, P)])
            pool.memset(onespad[:, :, :], 0.0).then_inc(pool_step, 1)
            pool.wait_ge(pool_step, steps[0] + 1)
            pool.memset(onespad[:, 0, 0:HD], 1.0)
            pool.memset(onespad[:, 1, HD:2 * HD], 1.0).then_inc(consts, 1)
            pool.wait_ge(ids_in, 32)
            with pool.Fori(0, NBATCH) as n:
                a = pool.value_load(ids[0:1, 1, bass.ds(n, 1)], min_val=0, max_val=NCOND2 - 1)
                pool.dma_start(ca_sb[:, :, bass.ds(R * n, R)], cond2_A[bass.ds(a, 1)].rearrange(
                    "a (p c) r -> p (a c) r", c=C)).then_inc(cond2_in, 16)
            for n in range(NBATCH):
                a = pool.value_load(ids[0:1, 1, n:n + 1], min_val=0, max_val=NCOND2 - 1)
                pool.dma_start(cb_sb[R * n:R * (n + 1), :],
                               cond2_B[bass.ds(a, 1)].rearrange("a r n -> (a r) n")).then_inc(cond2_in, 16)
            pool.wait_ge(fb_in, 32)
            fbv = fb_raw.rearrange("p (n i c) -> p i n c", i=NI, c=2)
            for q in range(4):
                last = pool.tensor_copy(fb_sb[:, 2 * q:2 * q + 2, :], fbv[:, 2 * q:2 * q + 2, :, 0])
            last.then_inc(fb_ready, 1)

            def prepare(i):
                for s in range(2):
                    n = bass.ds(2 * i + s, 1)
                    pool.tensor_tensor(kTm[s][:, :, :], kT_all[:, n, :].broadcast_to([P, G, P]),
                                       own[:, :].unsqueeze(2).broadcast_to([P, G, P]), ALU.mult)
                    pool.tensor_copy(qT[s][:, :, :], qT_all[:, n, :, :].rearrange("p n r t -> p (n r) t"))
                    v = vn[:, n, :, :].rearrange("p n (l e) d -> p (n l) e d", e=2)
                    o = vpad[s][:, :, :].rearrange("p (l e) d -> p l e d", e=2)
                    pool.tensor_copy(o[:, :, 0, 0:HD], v[:, :, 0, :])
                    pool.tensor_copy(o[:, :, 1, HD:2 * HD], v[:, :, 1, :]).then_inc(operands[s], 1)

            def masks(i):
                for u in range(4):
                    for s in range(2):
                        pool.wait_ge(exp_ready[s], 4 * i + u + 1)
                        pool.sem_inc(pool_passed, 1)
                        pt = PT[s][:, 2 * u:2 * u + 2, :].rearrange("p g (r q) -> p (g r) q", q=P)
                        pool.affine_select(out=pt, in_=pt, compare_op=ALU.is_ge, fill=0.0, base=0,
                                           pattern=[[0, 2 * REP], [1, P]], channel_multiplier=-1)\
                            .then_inc(pm_ready[s], 1)

            def residual(i):
                for s in range(2):
                    pool.wait_ge(xr_in[s], 16 * i + 16)
                    pool.tensor_tensor(xr[s][:, :], xr[s][:, :], bo_bc[:, :], ALU.add).then_inc(xb_ready[s], 1)

            pool.wait_ge(zeroed, 1)
            pool.wait_ge(bias_in, 48)
            pool.wait_ge(q_ready, NPAIR)
            pool.wait_ge(kv_ready, NPAIR)
            pool.wait_ge(kT_ready, 1)
            prepare(0)
            with pool.Fori(0, NPAIR - 1) as i:
                residual(i)
                masks(i)
                pool.wait_ge(pv_ps[1], i + 1)
                prepare(i + 1)
            residual(NPAIR - 1)
            masks(NPAIR - 1)

        @block.scalar
        def _(act):
            act.dma_start(wq_sb[:, :, :], Wq.rearrange("(p c) n -> p c n", c=C)).then_inc(w_in, 16)
            act.dma_start(wkv_sb[:, :, :], Wkv.rearrange("(p c) n -> p c n", c=C)).then_inc(w_in, 16)
            act.dma_start(b_sb[:, :], b.rearrange("(p c) -> p c", c=C)).then_inc(bias_in, 16)
            act.dma_start(bo_sb[:, :], bo.rearrange("(p c) -> p c", c=C)).then_inc(bias_in, 16)
            act.dma_start(bo_bc[:, :], bo.rearrange("(a n) -> a n", a=1).broadcast_to([P, D])).then_inc(bias_in, 16)
            for g in range(G):
                act.dma_start(wo_sb[HD * g:HD * (g + 1), :, :],
                              Wo.rearrange("(g r d) n -> g d r n", g=G, r=REP)[g]).then_inc(wo_in, 16)
            for j, job in enumerate(jobs):
                if j % 2:
                    act.wait_ge(pre_ps, j + 1)
                    src, dst = job_io(job)
                    act.activation(dst, src, ACT.Copy).then_inc(pre_out[1], 1)

            act.wait_ge(pre_ps, len(jobs))
            act.wait_ge(pre_out[0], (len(jobs) + 1) // 2)
            act.wait_ge(pre_out[1], len(jobs) // 2)
            act.wait_ge(fb_ready, 1)

            with act.Fori(0, NPAIR) as i:
                for s in range(2):
                    act.wait_ge(xT_ps, 2 * i + s + 1)
                    act.activation(xT[:, :, s, :], X[s][:, 0:512].rearrange("p (c t) -> p c t", c=C), ACT.Copy)\
                       .then_inc(xT_ready, 1)
                act.wait_ge(q_ps, i + 1)
                for r in range(REP):
                    last = act.activation(qT_all[:, bass.ds(2 * i, 2), r, :], X[0][:, 2 * r * P:2 * (r + 1) * P]
                                          .rearrange("p (s t) -> p s t", s=2), ACT.Identity, bias=bq[:, r:r + 1])
                last.then_inc(q_ready, 1)
            act.wait_ge(kT_ps, 1)
            act.activation(kT_all[:, :, :], X[0][:, :].rearrange("p (g t) -> p g t", g=G), ACT.Copy).then_inc(kT_ready, 1)

            with act.Fori(0, NPAIR) as i:
                for u in range(4):
                    for s in range(2):
                        act.wait_ge(st_ps[s], 4 * i + u + 1)
                        act.activation(PT[s][:, 2 * u:2 * u + 2, :], X[s][:, :].rearrange(
                            "p (g n) -> p g n", g=2), ACT.Exp, scale=SCALE).then_inc(exp_ready[s], 1)
                for s in range(2):
                    act.wait_ge(topk[s], i + 1)
                    act.activation(ex[s][:, :], rs[s][:, :], ACT.Exp, bias=nmax[s][:, :]).then_inc(gexp[s], 1)
                for s in range(2):
                    act.wait_ge(hGT_ps[s], i + 1)
                    act.activation(hGT[s][:, :, :], X[s][:, :].rearrange("p (i t) -> p i t", i=NI), ACT.Copy)\
                       .then_inc(hGT_ready[s], 1)

        @block.vector
        def _(dve):
            for s in range(2):
                dve.memset(vpad[s][:, :, :], 0.0)
                last = dve.memset(mT[s][:, :], 0.0)
            last.then_inc(zeroed, 1)
            dve.wait_ge(zeroed, 1)
            for j, job in enumerate(jobs):
                if j % 2 == 0:
                    dve.wait_ge(pre_ps, j + 1)
                    src, dst = job_io(job)
                    dve.tensor_copy(dst, src).then_inc(pre_out[0], 1)
            wait_jobs(dve, len(jobs))
            dve.wait_ge(consts, 1)
            dstep = sem("dstep")
            CHAIN = 9

            with dve.Fori(0, NPAIR) as i:
                dve.wait_ge(u_ps, i + 1)
                for s in range(2):
                    last = dve.tensor_scalar(uT[:, s, :], DN[0][:, s * P:(s + 1) * P],
                                             own2[:, bass.ds(2 * i + s, 1)], None, ALU.mult)
                last.then_inc(u_ready, 1)
                dve.wait_ge(kv_ps, i + 1)
                for s in range(2):
                    for t, o in enumerate((kn, vn)):
                        last = dve.tensor_tensor(
                            o[:, :, bass.ds(2 * i + s, 1), :].rearrange("p g j d -> p g (j d)"),
                            CX[s][:, t * P:(t + 1) * P].rearrange("p (g d) -> p g d", g=G),
                            bkv_bc[:, t * P:(t + 1) * P].rearrange("p (g d) -> p g d", g=G), ALU.add)
                last.then_inc(kv_ready, 1)
                dve.wait_ge(zx_ps, i + 1)
                for s in range(2):
                    last = dve.tensor_scalar(zx[:, bass.ds(2 * i + s, 1), :].rearrange("p n t -> p (n t)"),
                                             DN[1][:, s * P:(s + 1) * P], bz[:, 0:1],
                                             own[:, bass.ds(2 * i + s, 1)], ALU.add, ALU.mult)
                last.then_inc(zx_ready, 1)
            dve.wait_ge(zx_ready, NPAIR)

            with dve.Fori(0, NPAIR) as i:
                for u in range(REP):
                    for s in range(2):
                        dve.wait_ge(s_ps[s], 4 * i + u + 1)
                        dve.reduce_max(mx[s][:, u, :], X[s][:, :].rearrange("p (g k) -> p g k", g=G), AX_X)\
                           .then_inc(max_ready[s], 1)
                for s in range(2):
                    dve.wait_ge(max_ready[s], 4 * i + 4)
                    dve.tensor_scalar(mhl[s][:, :, :, 0], mx[s][:, :, :], -1.0, None, ALU.mult)\
                       .then_inc(mhi_ready[s], 1)
                for s in range(2):
                    dve.wait_ge(mhi_ready[s], i + 1)
                    dve.scalar_tensor_tensor(out=mhl[s][:, :, :, 1], in0=mx[s][:, :, :], scalar=-1.0,
                                             in1=mhl[s][:, :, :, 0], op0=ALU.mult, op1=ALU.subtract)\
                       .then_inc(m_ready[s], 1)
                for s in range(2):
                    dve.wait_ge(mT_ps[s], i + 1)
                    dve.tensor_copy(mT[s][0:2 * G, :], DN[s][0:2 * G, :]).then_inc(mT_ready[s], 1)
                for s in range(2):
                    dve.wait_ge(pv_ps[s], i + 1)
                    dve.reciprocal(rden[:, :], DN[s][:, :]).then_inc(rden_ready[s], 1)
                    dve.wait_ge(rden_ready[s], i + 1)
                    dve.tensor_tensor(ctxT[:, :, s, :], CX[s][:, :].rearrange("p (r t) -> p r t", r=REP),
                                      rden[:, :].rearrange("p (r t) -> p r t", r=REP), ALU.mult)\
                       .then_inc(ctx_ready[s], 1)
                    dve.wait_ge(ctx_ready[s], i + 1)
                dve.wait_ge(z_ps, i + 1)
                for s in range(2):
                    dve.scalar_tensor_tensor(out=zT[s][:, :], in0=DN[0][:, s * P:(s + 1) * P],
                                             scalar=own[:, bass.ds(2 * i + s, 1)],
                                             in1=zx[:, bass.ds(2 * i + s, 1), :].rearrange("p n t -> p (n t)"),
                                             op0=ALU.mult, op1=ALU.add).then_inc(z_ready[s], 1)

                def step(ins, s, n):
                    ins.then_inc(dstep, 1)
                    dve.wait_ge(dstep, 2 * CHAIN * i + CHAIN * s + n)
                    dve.sem_inc(dve_passed, 1)

                for s in range(2):
                    dve.wait_ge(r_ps[s], i + 1)
                    step(dve.tensor_copy(rs[s][:, :], DN[s][:, 256:256 + K]), s, 1)
                    step(dve.max(top[s][:, 0:8], rs[s][:, :]), s, 2)
                    dve.tensor_scalar(nmax[s][:, :], top[s][:, 0:1], -1.0, None, ALU.mult).then_inc(topk[s], 1)
                    step(dve.match_replace(rest[s][:, :], top[s][:, 0:8], rs[s][:, :], FAR), s, 3)
                    step(dve.max(top[s][:, 8:16], rest[s][:, :]), s, 4)
                    step(dve.match_replace(rest[s][:, :], top[s][:, 8:16], rest[s][:, :], FAR), s, 5)
                    step(dve.tensor_tensor(rest[s][:, :], rest[s][:, :], rs[s][:, :], ALU.not_equal), s, 6)
                    dve.wait_ge(gexp[s], i + 1)
                    step(dve.tensor_tensor_reduce(gate[s][:, :], ex[s][:, :], rest[s][:, :], 1.0, 0.0, ALU.mult,
                                                  ALU.add, gsum[s][:, 0:1]), s, 7)
                    step(dve.reciprocal(gsum[s][:, 1:2], gsum[s][:, 0:1]), s, 8)
                    step(dve.tensor_scalar(gate[s][:, :], gate[s][:, :], gsum[s][:, 1:2], FFN_SCALE,
                                           ALU.mult, ALU.mult), s, 9)
                    dve.wait_ge(h_ps[s], i + 1)
                    dve.tensor_tensor(hG[s].rearrange("p (r k) -> p r k", k=K),
                                      X[s][:, :].rearrange("p (r k) -> p r k", k=K),
                                      gate[s][:, :].unsqueeze(1).broadcast_to([P, RF, K]), ALU.mult)\
                       .then_inc(hG_ready[s], 1)
                for s in range(2):
                    dve.wait_ge(o_ps[s], i + 1)
                    dve.wait_ge(xb_ready[s], i + 1)
                    dve.tensor_tensor(fin[s][:, :], CX[s][:, :], xr[s][:, :], ALU.add).then_inc(fin_ready[s], 1)

        @block.tensor
        def _(pe):
            pe.wait_ge(consts, 1)
            pe.wait_ge(w_in, 48)
            for j, job in enumerate(jobs):
                kind, n, part = job
                o = bank[j % NB]
                if j >= NB:
                    pe.wait_ge(pre_out[j % 2], (j - NB) // 2 + 1)
                if kind == "fold":
                    if n == C and part == "q":
                        pe.wait_ge(lora_in, 32 * NBATCH)
                    if n == C + 1 and part == "q":
                        pe.wait_ge(bias_in, 48)
                    rhs = wq_sb if part == "q" else wkv_sb
                    for c in range(C):
                        if n < C:
                            lhsT = w_sb[:, c, n::C]
                        else:
                            lhsT = lb_sb[:, c, :] if n == C else b_sb[:, c:c + 1].broadcast_to([P, P])
                        last = pe.matmul(o[:, 0:rhs.shape[2]], lhsT, rhs[:, c, :], start=(c == 0), stop=(c == C - 1))
                elif kind == "bias_cols":
                    wait_jobs(pe, at[("fold", C + 1, "kv")] + 1)
                    for r in range(REP):
                        last = pe.matmul(o[:, r:r + 1], wf[0:1, C + 1, r * P:(r + 1) * P], ident[0:1, 0:1],
                                         start=True, stop=True)
                elif kind in ("cbT", "woT", "faT", "wrT"):
                    if kind == "cbT":
                        pe.wait_ge(cond2_in, 32 * NBATCH)
                    if kind == "woT" and n == 0:
                        pe.wait_ge(wo_in, 16 * G)
                    if kind == "faT" and n == 0:
                        pe.wait_ge(fa_in, 48)
                    rows = {"cbT": cb_sb[:, :], "woT": wo_sb[:, n % REP, :], "faT": fa_sb[:, n, :], "wrT": wr_sb[:, :]}[kind]
                    m = rows.shape[0]
                    for c in range(C):
                        last = pe.transpose(o[:, c * m:(c + 1) * m], rows[:, c::C], ident[0:m, 0:m])
                elif kind == "wob":
                    wait_jobs(pe, at[("woT", REP - 1)] + 1)
                    for r in range(REP):
                        for c in range(C):
                            last = pe.matmul(o[:, r * P:(r + 1) * P], woT[:, c, r, :], cbT[:, c, :],
                                             start=(c == 0), stop=(c == C - 1))
                elif kind == "bz":
                    for c in range(C):
                        last = pe.matmul(o[:, 0:1], cbT[:, c, :], bo_sb[:, c:c + 1], start=(c == 0), stop=(c == C - 1))
                else:
                    wait_jobs(pe, at[("wrT", 0)] + 1)
                    lo, hi = 512 * n, min(512 * n + 512, NH + K)
                    for c in range(C):
                        last = pe.matmul(o[:, 0:hi - lo], ca_sb[:, c, :], faT[:, c, lo:hi],
                                         start=(c == 0), stop=(c == C - 1))
                last.then_inc(pre_ps, 1)
            wait_jobs(pe, len(jobs))
            pe.wait_ge(zeroed, 1)

            with pe.Fori(0, NPAIR) as i:
                for s in range(2):
                    pe.wait_ge(x_in[s], 16 * i + 16)
                    for c in range(C):
                        last = pe.transpose(X[s][:, c * P:(c + 1) * P], xs[s][:, c::C], ident[:, :])
                    last.then_inc(xT_ps, 1)
                pe.wait_ge(xT_ready, 2 * i + 2)
                for c in range(C):
                    last = pe.matmul(DN[0][:, 0:2 * P], la_sb[:, c, :], xT[:, c, :, :], start=(c == 0), stop=(c == C - 1))
                last.then_inc(u_ps, 1)

                for r in range(REP):
                    o = X[0][:, 2 * r * P:(2 * r + 2) * P]
                    for c in range(C):
                        pe.matmul(o, wf[:, c, r * P:(r + 1) * P], xT[:, c, :, :], start=(c == 0), stop=False)
                    if r == 0:
                        pe.wait_ge(u_ready, i + 1)
                    last = pe.matmul(o, wf[:, C, r * P:(r + 1) * P], uT[:, :, :], start=False, stop=True)
                last.then_inc(q_ps, 1)
                for s in range(2):
                    for c in range(C):
                        pe.matmul(CX[s][:, 0:KV], xT[:, c, s, :], wf[:, c, D:D + KV], start=(c == 0), stop=False)
                    last = pe.matmul(CX[s][:, 0:KV], uT[:, s, :], wf[:, C, D:D + KV], start=False, stop=True)
                last.then_inc(kv_ps, 1)
                for c in range(C):
                    last = pe.matmul(DN[1][:, 0:2 * P], cbT[:, c, :], xT[:, c, :, :], start=(c == 0), stop=(c == C - 1))
                last.then_inc(zx_ps, 1)
                pe.wait_ge(q_ready, i + 1)
            pe.wait_ge(kv_ready, NPAIR)
            for g in range(G):
                last = pe.transpose(X[0][:, g * P:(g + 1) * P], kn[:, g, :, :].rearrange("p j d -> p (j d)"), ident[:, :])
            last.then_inc(kT_ps, 1)
            pe.wait_ge(kT_ready, 1)

            with pe.Fori(0, NPAIR) as i:
                for u in range(REP):
                    for s in range(2):
                        if u == 0:
                            pe.wait_ge(operands[s], i + 1)
                        else:
                            pe.wait_ge(max_ready[s], 4 * i + u)
                        for half in range(2):
                            o = X[s][:, half * 512:(half + 1) * 512]
                            pe.matmul(o, identb[:, :], causal[:, :, :], start=True, stop=False)
                            last = pe.matmul(o, qT[s][:, u, :], kTm[s][:, 4 * half:4 * half + 4, :],
                                             start=False, stop=True)
                        last.then_inc(s_ps[s], 1)
                for s in range(2):
                    pe.wait_ge(m_ready[s], i + 1)
                    for r in range(REP):
                        last = pe.matmul(DN[s][0:2 * G, r * P:(r + 1) * P], mhl[s][:, r, :, :], identb[:, :],
                                         start=True, stop=True)
                    last.then_inc(mT_ps[s], 1)
                for u in range(4):
                    for s in range(2):
                        if u == 0:
                            pe.wait_ge(mT_ready[s], i + 1)
                        else:
                            pe.wait_ge(exp_ready[s], 4 * i + u)
                        for j in range(2):
                            o, g = X[s][:, j * 512:(j + 1) * 512], 2 * u + j
                            pe.matmul(o, maxsel[:, g, :], mT[s][:, :], start=True, stop=False)
                            last = pe.matmul(o, kTm[s][:, g, :], qT[s][:, :, :], start=False, stop=True)
                        last.then_inc(st_ps[s], 1)
                for s in range(2):
                    pe.wait_ge(pm_ready[s], 4 * i + 4)
                    for o, v in ((CX[s], vpad[s]), (DN[s], None)):
                        for e in range(2):
                            for l in range(4):
                                lhsT = v[:, 2 * l + e, :] if v is not None else onespad[:, e, :]
                                last = pe.matmul(o[32 * l:32 * l + 32, :], lhsT, PT[s][:, 2 * l + e, :],
                                                 start=(e == 0), stop=(e == 1))
                    last.then_inc(pv_ps[s], 1)
                pe.wait_ge(ctx_ready[0], i + 1)
                pe.wait_ge(ctx_ready[1], i + 1)
                for r in range(REP):
                    last = pe.matmul(DN[0][:, 0:2 * P], wob[:, r, :], ctxT[:, r, :, :], start=(r == 0), stop=(r == REP - 1))
                last.then_inc(z_ps, 1)
                for s in range(2):
                    pe.wait_ge(z_ready[1], i + 1)
                    pe.matmul(DN[s][:, 256:256 + K], zT[s][:, :], mm[:, NH:NH + K], start=True, stop=True)\
                      .then_inc(r_ps[s], 1)
                    for half in range(2):
                        last = pe.matmul(X[s][:, half * 512:(half + 1) * 512], zT[s][:, :],
                                         mm[:, half * 512:(half + 1) * 512], start=True, stop=True)
                    last.then_inc(h_ps[s], 1)
                for s in range(2):
                    for r in range(REP):
                        pe.matmul(CX[s][:, :], ctxT[:, r, s, :], wo_sb[:, r, :], start=(r == 0), stop=False)
                for s in range(2):
                    pe.wait_ge(hG_ready[s], i + 1)
                    for n in range(NI):
                        last = pe.transpose(X[s][:, n * P:(n + 1) * P], hG[s][:, n * P:(n + 1) * P], ident[:, :])
                    last.then_inc(hGT_ps[s], 1)
                pe.wait_ge(fb_ready, 1)
                for s in range(2):
                    pe.wait_ge(hGT_ready[s], i + 1)
                    for n in range(NI):
                        last = pe.matmul(CX[s][:, :], hGT[s][:, n, :], fb_sb[:, n, :], start=False, stop=(n == NI - 1))
                    last.then_inc(o_ps[s], 1)


_INS = ['x', 'itok_B_14_62', 'itok_B_3_7', 'L0_cond_W', 'L0_cond_b', 'L0_cond_lora_A', 'L0_cond_lora_B',
        'L0_attn_Wq', 'L0_attn_Wkv', 'L0_attn_Wo', 'L0_attn_bo', 'L0_cond2_A', 'L0_cond2_B',
        'L0_ffn_A', 'L0_ffn_B', 'L0_ffn_Wr']
_OUTS = [((8, 128, 512), 'float32')]


def kernel(**inputs):
    import numpy as _np
    import concourse.bacc as _bacc
    from concourse import mybir as _mybir
    from concourse.bass_utils import run_bass_kernel_spmd as _run

    nc = _bacc.Bacc("TRN2", target_bir_lowering=False, num_devices=1)
    arrays, args = {}, []
    for name in _INS:
        a = _np.ascontiguousarray(inputs[name])
        arrays[f"in_{name}_dram"] = a
        args.append(nc.dram_tensor(f"in_{name}_dram", a.shape, _mybir.dt.from_np(a.dtype), kind="ExternalInput").ap())
    for i, (shape, dtype) in enumerate(_OUTS):
        dt = _mybir.dt.from_np(_np.dtype(dtype))
        args.append(nc.dram_tensor(f"out_{i}_dram", shape, dt, kind="ExternalOutput").ap())
    adaln_attn_ffn_kernel(nc, *args)
    r = _run(nc, [arrays], core_ids=[0])
    return r.results[0]["out_0_dram"]
```

```python
from contextlib import ExitStack

import concourse.bass as bass
from concourse import mybir

F32 = mybir.dt.float32
F32R = mybir.dt.float32r
BF16 = mybir.dt.bfloat16
I32 = mybir.dt.int32
ALU = mybir.AluOpType
ACT = mybir.ActivationFunctionType
AX_X = mybir.AxisListType.X

P = 128


def adaln_attn_ffn_kernel(nc, x, cond_ids, cond2_ids, W, b, lora_A, lora_B, Wq, Wkv, Wo, bo,
                          cond2_A, cond2_B, ffn_A, ffn_B, Wr, out):
    NBATCH, T, D = x.shape
    NPAIR = NBATCH // 2
    R = lora_A.shape[2]
    NLORA, NCOND2 = lora_A.shape[0], cond2_A.shape[0]
    KV = Wkv.shape[1]
    H, G, HD = 32, 8, 16
    REP = H // G
    C = D // P
    K, RF, _ = ffn_A.shape
    NI = K * RF // P
    NH = K * RF
    TOP8 = 2
    SCALE = float(HD) ** -0.5
    LORA_SCALE, FFN_SCALE = 2.0, 2.0
    FAR = -3.0e38
    assert T == P and NBATCH * R == P and G * HD == P and C == REP == 4 and 2 * K == P

    with ExitStack() as ctx:
        def sb(name, shape, dt=F32):
            return ctx.enter_context(nc.sbuf_tensor(name, shape, dt))

        def sem(name):
            return ctx.enter_context(nc.semaphore(name))

        def sems(name):
            return [sem(f"{name}{s}") for s in range(2)]

        ident = sb("ident", [P, P])
        identb = sb("identb", [P, P], BF16)
        causal = sb("causal", [P, 4, P], BF16)
        own = sb("own", [P, NBATCH])
        own2 = sb("own2", [P, NBATCH])
        odd = sb("odd", [P, 2])
        maxsel = sb("maxsel", [P, G])
        onespad = sb("onespad", [P, 2, 32])
        w_sb = sb("w_sb", [P, C, D])
        wq_sb = sb("wq_sb", [P, C, D])
        wkv_sb = sb("wkv_sb", [P, C, KV])
        wo_sb = sb("wo_sb", [P, REP, D])
        b_sb = sb("b_sb", [P, C])
        bo_sb = sb("bo_sb", [P, C])
        bo_bc = sb("bo_bc", [P, D])
        ids = sb("ids", [1, 2, NBATCH], I32)
        la_sb = sb("la_sb", [P, C, NBATCH * R])
        lb_sb = sb("lb_sb", [P, C, NBATCH * R])
        ca_sb = sb("ca_sb", [P, C, NBATCH * R])
        cb_sb = sb("cb_sb", [P, D])
        fa_sb = sb("fa_sb", [P, NI, D])
        PT_fb = sb("PT_fb", [P, 2 * G * 4 * P])
        fb_raw = PT_fb[:, 0:D * RF]
        wr_sb = sb("wr_sb", [K, D])
        wf = sb("wf", [P, C + 2, D + KV])
        bq = sb("bq", [P, REP])
        bkv_bc = wf[:, C + 1, D:D + KV]
        cbT = sb("cbT", [P, C, P])
        woT = sb("woT", [P, C, REP, P])
        wob = sb("wob", [P, REP, P])
        bz = sb("bz", [P, 1])
        faT = sb("faT", [P, C, NH + K])
        mm = sb("mm", [P, NH + K])
        fb_sb = sb("fb_sb", [P, NI, D])
        xs = [sb(f"xs{s}", [P, D]) for s in range(2)]
        xr = [sb(f"xr{s}", [P, D]) for s in range(2)]
        xT = sb("xT", [P, C, 2, P])
        uT = sb("uT", [P, 2, P])
        w_flat, wq_flat = w_sb[:, :, :].rearrange("p c n -> p (c n)"), wq_sb[:, :, :].rearrange("p c n -> p (c n)")
        q_parts = sb("q_parts", [P, 2, 2, REP * P])
        q_flat = q_parts[:, :, :, :].rearrange("p a s n -> p (a s n)")
        kn = w_flat[:, 0:G * P].rearrange("p (g j d) -> p g j d", g=G, j=G)
        vn = w_flat[:, G * P:2 * G * P].rearrange("p (g j d) -> p g j d", g=G, j=G)
        k_parts = [t.rearrange("p (g e t) -> p g e t", g=G, e=2) for t in (wq_flat, q_flat)]
        zx = wkv_sb[:, :, :].rearrange("p c n -> p (c n)").rearrange("p (n t) -> p n t", n=NBATCH)
        QX = [sb(f"QX{s}", [P, G // 2, REP * P], F32R) for s in range(2)]
        KX = [sb(f"KX{s}", [P, G, P], F32R) for s in range(2)]
        vpad = [sb(f"vpad{s}", [P, G, 32]) for s in range(2)]
        q_dram = nc.dram_tensor("q_dram", [2, NBATCH, P, REP * P], F32, kind="Internal").ap()
        k_dram = nc.dram_tensor("k_dram", [2, G, P, 2, P], F32, kind="Internal").ap()
        mx = [sb(f"mx{s}", [P, REP, G]) for s in range(2)]
        mhl = [sb(f"mhl{s}", [P, REP, G, 2], BF16) for s in range(2)]
        PT = [PT_fb[:, s * G * 4 * P:(s + 1) * G * 4 * P].rearrange("p (g n) -> p g n", g=G) for s in range(2)]
        rden, ctxT, fin = cb_sb, xT, xs
        zT = [uT[:, s, :] for s in range(2)]
        rs = [sb(f"rs{s}", [P, K]) for s in range(2)]
        rest = [sb(f"rest{s}", [P, K]) for s in range(2)]
        top = [sb(f"top{s}", [P, 8 * TOP8]) for s in range(2)]
        nmax = [sb(f"nmax{s}", [P, 1]) for s in range(2)]
        ex = [sb(f"ex{s}", [P, K]) for s in range(2)]
        gate = [sb(f"gate{s}", [P, K]) for s in range(2)]
        gsum = [sb(f"gsum{s}", [P, 2]) for s in range(2)]
        faT_flat = faT[:, :, :].rearrange("p c n -> p (c n)")
        hG = [faT_flat[:, s * NH:(s + 1) * NH] for s in range(2)]
        hGT = [faT_flat[:, (2 + s) * NH:(3 + s) * NH].rearrange("p (i t) -> p i t", i=NI) for s in range(2)]

        X = [ctx.enter_context(nc.psum_tensor(f"X{s}", [P, 1024], F32)) for s in range(2)]
        CX = [ctx.enter_context(nc.psum_tensor(f"CX{s}", [P, 512], F32)) for s in range(2)]
        DN = [ctx.enter_context(nc.psum_tensor(f"DN{s}", [P, 512], F32)) for s in range(2)]
        bank = [X[0][:, 0:512], X[0][:, 512:1024], X[1][:, 0:512], X[1][:, 512:1024],
                CX[0][:, :], CX[1][:, :], DN[0][:, :], DN[1][:, :]]
        NB = len(bank)

        consts = sem("consts")
        pool_step = sem("pool_step")
        zeroed = sem("zeroed")
        dve_passed, pool_passed = sem("dve_passed"), sem("pool_passed")
        ids_in = sem("ids_in")
        w_in = sem("w_in")
        bias_in = sem("bias_in")
        lora_in = sem("lora_in")
        cond2_in = sem("cond2_in")
        wo_in = sem("wo_in")
        fa_in = sem("fa_in")
        fb_in = sem("fb_in")
        fb_ready = sem("fb_ready")
        pre_ps = sem("pre_ps")
        pre_out = [sem("pre_dve"), sem("pre_act")]
        x_in = sems("x_in")
        xr_in = sems("xr_in")
        xT_ps, xT_ready = sem("xT_ps"), sem("xT_ready")
        u_ps, u_ready = sem("u_ps"), sem("u_ready")
        kv_ps, kv_ready, zx_ps, zx_ready = sem("kv_ps"), sem("kv_ready"), sem("zx_ps"), sem("zx_ready")
        kT_ps, khigh_ready, klow_ready, k_stored = sem("kT_ps"), sem("khigh_ready"), sem("klow_ready"), sem("k_stored")
        q_ps, qhigh_ready, qlow_ready, q_stored = sem("q_ps"), sem("qhigh_ready"), sem("qlow_ready"), sem("q_stored")
        qk_in, vpad_ready = sems("qk_in"), sems("vpad_ready")
        s_ps, max_ready, mhi_ready, m_ready = sems("s_ps"), sems("max_ready"), sems("mhi_ready"), sems("m_ready")
        mT_ps, mT_ready = sems("mT_ps"), sems("mT_ready")
        st_ps, exp_ready, pm_ready = sems("st_ps"), sems("exp_ready"), sems("pm_ready")
        den_ps, pv_ps, rden_ready, ctx_ready = sems("den_ps"), sems("pv_ps"), sems("rden_ready"), sems("ctx_ready")
        z_ps, z_ready = sems("z_ps"), sems("z_ready")
        r_ps, h_ps = sems("r_ps"), sems("h_ps")
        topk, gexp = sems("topk"), sems("gexp")
        hG_ready, hGT_ps, hGT_ready = sems("hG_ready"), sems("hGT_ps"), sems("hGT_ready")
        o_ps, xb_ready, fin_ready, stored = sems("o_ps"), sems("xb_ready"), sems("fin_ready"), sems("stored")

        fold = [("fold", c, part) for c in range(C + 2) for part in ("q", "kv")]
        jobs = fold + [("bias_cols", 0, ""), ("cbT", 0, ""), ("bz", 0, "")]
        NFIRST = len(jobs)
        jobs += [("woT", r, "") for r in range(REP)] + [("faT", i, "") for i in range(NI)] + [("wrT", 0, "")]
        jobs += [("wob", 0, "")] + [("mm", n, "") for n in range(3)]
        at = {job[:2] if job[0] != "fold" else job: j for j, job in enumerate(jobs)}

        def job_bank(j):
            return bank[j % NB] if j < NFIRST else bank[(j - NFIRST + 2) % NB]

        def job_io(job):
            kind, n, part = job
            o = job_bank(at[job if kind == "fold" else job[:2]])
            if kind == "fold" and part == "q":
                return (o.rearrange("p (g r d) -> p r g d", g=G, r=REP),
                        wf[:, n, 0:D].rearrange("p (r g d) -> p r g d", r=REP, g=G))
            if kind == "fold":
                return (o[:, 0:KV].rearrange("p (g t d) -> p t g d", g=G, t=2),
                        wf[:, n, D:D + KV].rearrange("p (t g d) -> p t g d", t=2, g=G))
            if kind == "bias_cols":
                return o[:, 0:REP], bq[:, :]
            if kind == "cbT":
                return o.rearrange("p (c n) -> p c n", c=C), cbT[:, :, :]
            if kind == "woT":
                return o.rearrange("p (c n) -> p c n", c=C), woT[:, :, n, :]
            if kind == "faT":
                return o.rearrange("p (c n) -> p c n", c=C), faT[:, :, n * P:(n + 1) * P]
            if kind == "wrT":
                return o[:, 0:C * K].rearrange("p (c n) -> p c n", c=C), faT[:, :, NH:NH + K]
            if kind == "wob":
                return o.rearrange("p (r n) -> p r n", r=REP), wob[:, :, :]
            if kind == "bz":
                return o[:, 0:1], bz[:, :]
            lo, hi = 512 * n, min(512 * n + 512, NH + K)
            return o[:, 0:hi - lo], mm[:, lo:hi]

        def wait_jobs(eng, n):
            eng.wait_ge(pre_out[0], (n + 1) // 2)
            eng.wait_ge(pre_out[1], n // 2)

        block = ctx.enter_context(nc.Block())

        @block.sync
        def _(sp):
            sp.dma_start(ids[:, 0, :], cond_ids.rearrange("(a n) -> a n", a=1)).then_inc(ids_in, 16)
            sp.dma_start(ids[:, 1, :], cond2_ids.rearrange("(a n) -> a n", a=1)).then_inc(ids_in, 16)
            sp.dma_start(w_sb[:, :, :], W.rearrange("(p c) n -> p c n", c=C)).then_inc(w_in, 16)
            for s in range(2):
                sp.dma_start(xs[s][:, :], x[s]).then_inc(x_in[s], 16)
            sp.wait_ge(ids_in, 32)
            with sp.Fori(0, NBATCH) as n:
                a = sp.value_load(ids[0:1, 0, bass.ds(n, 1)], min_val=0, max_val=NLORA - 1)
                sp.dma_start(lb_sb[:, :, bass.ds(R * n, R)], lora_B[bass.ds(a, 1)].rearrange(
                    "a (p c) r -> p (a c) r", c=C)).then_inc(lora_in, 16)
                sp.dma_start(la_sb[:, :, bass.ds(R * n, R)], lora_A[bass.ds(a, 1)].rearrange(
                    "a (p c) r -> p (a c) r", c=C)).then_inc(lora_in, 16)
            sp.dma_start(wr_sb[:, :], Wr).then_inc(fa_in, 16)
            for c2 in range(2):
                sp.dma_start(fa_sb[K * c2:K * (c2 + 1), :, :],
                             ffn_A.rearrange("k (i c) n -> c k i n", c=2)[c2]).then_inc(fa_in, 16)
            fbv = ffn_B.rearrange("k n r -> k (n r)")
            sp.dma_start(fb_raw[0:K, :], fbv).then_inc(fb_in, 16)
            sp.dma_start(fb_raw[K:2 * K, 0:D * RF - 1], fbv[:, 1:D * RF]).then_inc(fb_in, 16)
            sp.sem_inc(q_stored, 16)

            def store_q(i):
                sp.wait_ge(qlow_ready, i + 1)
                for a in range(2):
                    sp.dma_start(q_dram[a, bass.ds(2 * i, 2)].rearrange("n p f -> p n f"), q_parts[:, a, :, :])\
                      .then_inc(q_stored, 16)

            with sp.Fori(0, NPAIR - 1) as i:
                sp.wait_ge(xT_ps, 2 * i + 2)
                for s in range(2):
                    sp.dma_start(xs[s][:, :], x[bass.ds(2 * i + 2 + s, 1)].rearrange("a t n -> (a t) n"))\
                      .then_inc(x_in[s], 16)
                store_q(i)
            store_q(NPAIR - 1)
            sp.wait_ge(khigh_ready, 1)
            sp.dma_start(k_dram[0].rearrange("g p e t -> p g e t"), k_parts[0]).then_inc(k_stored, 16)
            sp.wait_ge(klow_ready, 1)
            sp.dma_start(k_dram[1].rearrange("g p e t -> p g e t"), k_parts[1]).then_inc(k_stored, 16)
            for s in range(2):
                sp.dma_start(xr[s][:, :], x[s]).then_inc(xr_in[s], 16)

            def load_qk(i, s):
                for a, (qa, ka) in enumerate(((0, 0), (0, 1), (1, 0))):
                    rows, n = slice(32 * a, 32 * a + 32), bass.ds(2 * i + s, 1)
                    sp.dma_start(QX[s][rows, :, :].bitcast(F32),
                                 q_dram[qa, n].rearrange("n (j x) f -> x (n j) f", x=32)).then_inc(qk_in[s], 16)
                    sp.dma_start(KX[s][rows, :, :].bitcast(F32).rearrange("x (j e) t -> x j (e t)", e=2),
                                 k_dram[ka, n].rearrange("n (j x) e t -> x (n j) (e t)", x=32)).then_inc(qk_in[s], 16)

            sp.wait_ge(q_stored, 32 * NPAIR + 16)
            sp.wait_ge(k_stored, 32)
            for s in range(2):
                load_qk(0, s)

            def store(i, s):
                sp.wait_ge(fin_ready[s], i + 1)
                sp.dma_start(out[bass.ds(2 * i + s, 1)].rearrange("a t n -> (a t) n"), fin[s][:, :])\
                  .then_inc(stored[s], 16)

            with sp.Fori(0, NPAIR - 1) as i:
                for s in range(2):
                    sp.wait_ge(st_ps[s], 4 * i + 4)
                    load_qk(i + 1, s)
                for s in range(2):
                    store(i, s)
                    sp.dma_start(xr[s][:, :], x[bass.ds(2 * i + 2 + s, 1)].rearrange("a t n -> (a t) n"))\
                      .then_inc(xr_in[s], 16)
            for s in range(2):
                store(NPAIR - 1, s)
            for s in range(2):
                sp.wait_ge(stored[s], 16 * NPAIR)

        @block.gpsimd
        def _(pool):
            steps = [0]

            def then_wait(ins):
                steps[0] += 1
                ins.then_inc(pool_step, 1)
                pool.wait_ge(pool_step, steps[0])

            def band(t, low, high, pattern):
                then_wait(pool.memset(t, 1.0))
                then_wait(pool.affine_select(out=t, in_=t, compare_op=ALU.is_ge, fill=0.0, base=-low,
                                             pattern=[[-a, n] for a, n in pattern], channel_multiplier=1))
                then_wait(pool.affine_select(out=t, in_=t, compare_op=ALU.is_ge, fill=0.0, base=high,
                                             pattern=[[a, n] for a, n in pattern], channel_multiplier=-1))

            band(ident[:, :], 0, 0, [(1, P)])
            then_wait(pool.tensor_copy(identb[:, :], ident[:, :]))
            band(own[:, :], 0, R - 1, [(R, NBATCH)])
            then_wait(pool.tensor_scalar(own2[:, :], own[:, :], LORA_SCALE, None, ALU.mult))
            then_wait(pool.memset(causal[:, :, :], 0.0))
            then_wait(pool.affine_select(out=causal[:, :, :], in_=causal[:, :, :], compare_op=ALU.is_ge,
                                         fill=FAR, base=0, pattern=[[0, 4], [-1, P]], channel_multiplier=1))
            band(maxsel[:, :], 3 * 32, 3 * 32 + 1, [(2, G)])
            then_wait(pool.tensor_tensor(odd[:, 0:1], own[:, 0:1], own[:, 2:3], ALU.add))
            for n in (4, 6):
                then_wait(pool.tensor_tensor(odd[:, 0:1], odd[:, 0:1], own[:, n:n + 1], ALU.add))
            then_wait(pool.tensor_scalar(odd[:, 1:2], odd[:, 0:1], -1.0, 1.0, ALU.mult, ALU.add))
            pool.memset(onespad[:, :, :], 0.0).then_inc(pool_step, 1)
            pool.wait_ge(pool_step, steps[0] + 1)
            pool.memset(onespad[:, 0, 0:HD], 1.0)
            pool.memset(onespad[:, 1, HD:2 * HD], 1.0).then_inc(consts, 1)
            pool.wait_ge(ids_in, 32)
            with pool.Fori(0, NBATCH) as n:
                a = pool.value_load(ids[0:1, 1, bass.ds(n, 1)], min_val=0, max_val=NCOND2 - 1)
                pool.dma_start(ca_sb[:, :, bass.ds(R * n, R)], cond2_A[bass.ds(a, 1)].rearrange(
                    "a (p c) r -> p (a c) r", c=C)).then_inc(cond2_in, 16)
            for n in range(NBATCH):
                a = pool.value_load(ids[0:1, 1, n:n + 1], min_val=0, max_val=NCOND2 - 1)
                pool.dma_start(cb_sb[R * n:R * (n + 1), :],
                               cond2_B[bass.ds(a, 1)].rearrange("a r n -> (a r) n")).then_inc(cond2_in, 16)
            pool.wait_ge(fb_in, 32)
            fbv = fb_raw.rearrange("p (n i c) -> p i n c", i=NI, c=2)
            for q in range(4):
                last = pool.tensor_copy(fb_sb[:, 2 * q:2 * q + 2, :], fbv[:, 2 * q:2 * q + 2, :, 0])
            last.then_inc(fb_ready, 1)

            def prepare(i):
                for s in range(2):
                    v = vn[:, bass.ds(2 * i + s, 1), :, :].rearrange("p n (l e) d -> p (n l) e d", e=2)
                    o = vpad[s][:, :, :].rearrange("p (l e) d -> p l e d", e=2)
                    pool.tensor_copy(o[:, :, 0, 0:HD], v[:, :, 0, :])
                    pool.tensor_copy(o[:, :, 1, HD:2 * HD], v[:, :, 1, :]).then_inc(vpad_ready[s], 1)

            def masks(i):
                for u in range(4):
                    for s in range(2):
                        pool.wait_ge(exp_ready[s], 4 * i + u + 1)
                        pool.sem_inc(pool_passed, 1)
                        pt = PT[s][:, 2 * u:2 * u + 2, :].rearrange("p g (r q) -> p (g r) q", q=P)
                        pool.affine_select(out=pt, in_=pt, compare_op=ALU.is_ge, fill=0.0, base=0,
                                           pattern=[[0, 2 * REP], [1, P]], channel_multiplier=-1)\
                            .then_inc(pm_ready[s], 1)

            def residual(i):
                for s in range(2):
                    pool.wait_ge(xr_in[s], 16 * i + 16)
                    pool.tensor_tensor(xr[s][:, :], xr[s][:, :], bo_bc[:, :], ALU.add).then_inc(xb_ready[s], 1)

            pool.wait_ge(zeroed, 1)
            pool.wait_ge(bias_in, 48)
            pool.wait_ge(kv_ready, NPAIR)
            prepare(0)
            masks(0)
            with pool.Fori(0, NPAIR - 1) as i:
                residual(i)
                pool.wait_ge(pv_ps[1], i + 1)
                prepare(i + 1)
                masks(i + 1)
            residual(NPAIR - 1)

        @block.scalar
        def _(act):
            act.dma_start(wq_sb[:, :, :], Wq.rearrange("(p c) n -> p c n", c=C)).then_inc(w_in, 16)
            act.dma_start(wkv_sb[:, :, :], Wkv.rearrange("(p c) n -> p c n", c=C)).then_inc(w_in, 16)
            act.dma_start(b_sb[:, :], b.rearrange("(p c) -> p c", c=C)).then_inc(bias_in, 16)
            act.dma_start(bo_sb[:, :], bo.rearrange("(p c) -> p c", c=C)).then_inc(bias_in, 16)
            act.dma_start(bo_bc[:, :], bo.rearrange("(a n) -> a n", a=1).broadcast_to([P, D])).then_inc(bias_in, 16)
            for g in range(G):
                act.dma_start(wo_sb[HD * g:HD * (g + 1), :, :],
                              Wo.rearrange("(g r d) n -> g d r n", g=G, r=REP)[g]).then_inc(wo_in, 16)

            def act_jobs(first, end):
                for j in range(first, end):
                    if j % 2:
                        act.wait_ge(pre_ps, j + 1)
                        src, dst = job_io(jobs[j])
                        act.activation(dst, src, ACT.Copy).then_inc(pre_out[1], 1)

            act_jobs(0, NFIRST)
            wait_jobs(act, NFIRST)

            with act.Fori(0, NPAIR) as i:
                for s in range(2):
                    act.wait_ge(xT_ps, 2 * i + s + 1)
                    act.activation(xT[:, :, s, :], X[s][:, 0:512].rearrange("p (c t) -> p c t", c=C), ACT.Copy)\
                       .then_inc(xT_ready, 1)
                act.wait_ge(q_ps, i + 1)
                act.wait_ge(q_stored, 32 * i + 16)
                for r in range(REP):
                    act.activation(q_parts[:, 0, :, r * P:(r + 1) * P].bitcast(F32R),
                                   X[0][:, 2 * r * P:2 * (r + 1) * P].rearrange("p (s t) -> p s t", s=2),
                                   ACT.Identity, bias=bq[:, r:r + 1]).then_inc(qhigh_ready, 1)
            act.wait_ge(kT_ps, 1)
            for e in range(2):
                last = act.activation(k_parts[0][:, :, e, :].bitcast(F32R), X[0][:, :].rearrange("p (g t) -> p g t", g=G),
                                      ACT.Copy, scale=odd[:, e:e + 1])
            last.then_inc(khigh_ready, 1)
            act_jobs(NFIRST, len(jobs))
            act.wait_ge(fb_ready, 1)

            def numerators(i):
                for u in range(4):
                    for s in range(2):
                        act.wait_ge(st_ps[s], 4 * i + u + 1)
                        act.activation(PT[s][:, 2 * u:2 * u + 2, :], X[s][:, :].rearrange(
                            "p (g n) -> p g n", g=2), ACT.Exp, scale=SCALE).then_inc(exp_ready[s], 1)

            def experts(i):
                for s in range(2):
                    act.wait_ge(topk[s], i + 1)
                    act.activation(ex[s][:, :], rs[s][:, :], ACT.Exp, bias=nmax[s][:, :]).then_inc(gexp[s], 1)
                for s in range(2):
                    act.wait_ge(hGT_ps[s], i + 1)
                    act.activation(hGT[s][:, :, :], X[s][:, :].rearrange("p (i t) -> p i t", i=NI), ACT.Copy)\
                       .then_inc(hGT_ready[s], 1)

            numerators(0)
            with act.Fori(0, NPAIR - 1) as i:
                experts(i)
                numerators(i + 1)
            experts(NPAIR - 1)

        @block.vector
        def _(dve):
            for s in range(2):
                dve.memset(vpad[s][:, :, :], 0.0)
                last = dve.memset(QX[s][96:128, :, :].bitcast(F32), 0.0)
            last.then_inc(zeroed, 1)

            def dve_jobs(first, end):
                for j in range(first, end):
                    if j % 2 == 0:
                        dve.wait_ge(pre_ps, j + 1)
                        src, dst = job_io(jobs[j])
                        dve.tensor_copy(dst, src).then_inc(pre_out[0], 1)

            dve_jobs(0, NFIRST)
            wait_jobs(dve, NFIRST)
            dve.wait_ge(consts, 1)
            for s in range(2):
                last = dve.tensor_copy(KX[s][96:128, :, :], maxsel[96:128, :].unsqueeze(2).broadcast_to([32, G, P]))
            last.then_inc(zeroed, 1)
            dstep = sem("dstep")
            CHAIN = 9

            with dve.Fori(0, NPAIR) as i:
                dve.wait_ge(u_ps, i + 1)
                for s in range(2):
                    last = dve.tensor_scalar(uT[:, s, :], DN[0][:, s * P:(s + 1) * P],
                                             own2[:, bass.ds(2 * i + s, 1)], None, ALU.mult)
                last.then_inc(u_ready, 1)
                for r in range(REP):
                    dve.wait_ge(qhigh_ready, 4 * i + r - r % 2 + 2)
                    last = dve.scalar_tensor_tensor(
                        out=q_parts[:, 1, :, r * P:(r + 1) * P].bitcast(F32R),
                        in0=X[0][:, 2 * r * P:2 * (r + 1) * P].rearrange("p (s t) -> p s t", s=2),
                        scalar=bq[:, r:r + 1], in1=q_parts[:, 0, :, r * P:(r + 1) * P],
                        op0=ALU.add, op1=ALU.subtract)
                last.then_inc(qlow_ready, 1)
                dve.wait_ge(kv_ps, i + 1)
                for s in range(2):
                    for t, o in enumerate((kn, vn)):
                        last = dve.tensor_tensor(
                            o[:, :, bass.ds(2 * i + s, 1), :].rearrange("p g j d -> p g (j d)"),
                            CX[s][:, t * P:(t + 1) * P].rearrange("p (g d) -> p g d", g=G),
                            bkv_bc[:, t * P:(t + 1) * P].rearrange("p (g d) -> p g d", g=G), ALU.add)
                last.then_inc(kv_ready, 1)
                dve.wait_ge(zx_ps, i + 1)
                for s in range(2):
                    last = dve.tensor_scalar(zx[:, bass.ds(2 * i + s, 1), :].rearrange("p n t -> p (n t)"),
                                             DN[1][:, s * P:(s + 1) * P], bz[:, 0:1],
                                             own[:, bass.ds(2 * i + s, 1)], ALU.add, ALU.mult)
                last.then_inc(zx_ready, 1)
            dve.wait_ge(zx_ready, NPAIR)
            dve.wait_ge(khigh_ready, 1)
            dve.wait_ge(q_stored, 32 * NPAIR + 16)
            for e in range(2):
                last = dve.scalar_tensor_tensor(
                    out=k_parts[1][:, :, e, :].bitcast(F32R), in0=X[0][:, :].rearrange("p (g t) -> p g t", g=G),
                    scalar=odd[:, e:e + 1], in1=k_parts[0][:, :, e, :], op0=ALU.mult, op1=ALU.subtract)
            last.then_inc(klow_ready, 1)
            dve_jobs(NFIRST, len(jobs))
            wait_jobs(dve, len(jobs))

            def maxima(i):
                for u in range(REP):
                    for s in range(2):
                        dve.wait_ge(s_ps[s], 4 * i + u + 1)
                        dve.reduce_max(mx[s][:, u, :], X[s][:, :].rearrange("p (g k) -> p g k", g=G), AX_X)\
                           .then_inc(max_ready[s], 1)
                for s in range(2):
                    dve.wait_ge(max_ready[s], 4 * i + 4)
                    dve.tensor_scalar(mhl[s][:, :, :, 0], mx[s][:, :, :], -1.0, None, ALU.mult)\
                       .then_inc(mhi_ready[s], 1)
                for s in range(2):
                    dve.wait_ge(mhi_ready[s], i + 1)
                    dve.scalar_tensor_tensor(out=mhl[s][:, :, :, 1], in0=mx[s][:, :, :], scalar=-1.0,
                                             in1=mhl[s][:, :, :, 0], op0=ALU.mult, op1=ALU.subtract)\
                       .then_inc(m_ready[s], 1)
                for s in range(2):
                    dve.wait_ge(mT_ps[s], i + 1)
                    for j in range(G // 2):
                        dve.tensor_copy(QX[s][96:96 + 2 * G, j, :], DN[s][96:96 + 2 * G, :]).then_inc(mT_ready[s], 1)

            def context_and_gates(i):
                for s in range(2):
                    dve.wait_ge(den_ps[s], i + 1)
                    dve.reciprocal(rden[:, :], DN[s][:, :]).then_inc(rden_ready[s], 1)
                    dve.wait_ge(rden_ready[s], i + 1)
                    dve.wait_ge(pv_ps[s], i + 1)
                    dve.tensor_tensor(ctxT[:, :, s, :], CX[s][:, :].rearrange("p (r t) -> p r t", r=REP),
                                      rden[:, :].rearrange("p (r t) -> p r t", r=REP), ALU.mult)\
                       .then_inc(ctx_ready[s], 1)
                    dve.wait_ge(ctx_ready[s], i + 1)
                for s in range(2):
                    dve.wait_ge(z_ps[s], i + 1)
                    dve.scalar_tensor_tensor(out=zT[s], in0=DN[s][:, 0:P],
                                             scalar=own[:, bass.ds(2 * i + s, 1)],
                                             in1=zx[:, bass.ds(2 * i + s, 1), :].rearrange("p n t -> p (n t)"),
                                             op0=ALU.mult, op1=ALU.add).then_inc(z_ready[s], 1)

                def step(ins, s, n):
                    ins.then_inc(dstep, 1)
                    dve.wait_ge(dstep, 2 * CHAIN * i + CHAIN * s + n)
                    dve.sem_inc(dve_passed, 1)

                for s in range(2):
                    dve.wait_ge(r_ps[s], i + 1)
                    step(dve.tensor_copy(rs[s][:, :], DN[s][:, 256:256 + K]), s, 1)
                    step(dve.max(top[s][:, 0:8], rs[s][:, :]), s, 2)
                    dve.tensor_scalar(nmax[s][:, :], top[s][:, 0:1], -1.0, None, ALU.mult).then_inc(topk[s], 1)
                    step(dve.match_replace(rest[s][:, :], top[s][:, 0:8], rs[s][:, :], FAR), s, 3)
                    step(dve.max(top[s][:, 8:16], rest[s][:, :]), s, 4)
                    step(dve.match_replace(rest[s][:, :], top[s][:, 8:16], rest[s][:, :], FAR), s, 5)
                    step(dve.tensor_tensor(rest[s][:, :], rest[s][:, :], rs[s][:, :], ALU.not_equal), s, 6)
                    dve.wait_ge(gexp[s], i + 1)
                    step(dve.tensor_tensor_reduce(gate[s][:, :], ex[s][:, :], rest[s][:, :], 1.0, 0.0, ALU.mult,
                                                  ALU.add, gsum[s][:, 0:1]), s, 7)
                    step(dve.reciprocal(gsum[s][:, 1:2], gsum[s][:, 0:1]), s, 8)
                    step(dve.tensor_scalar(gate[s][:, :], gate[s][:, :], gsum[s][:, 1:2], FFN_SCALE,
                                           ALU.mult, ALU.mult), s, 9)
                    dve.wait_ge(h_ps[s], i + 1)
                    dve.tensor_tensor(hG[s].rearrange("p (r k) -> p r k", k=K),
                                      X[s][:, :].rearrange("p (r k) -> p r k", k=K),
                                      gate[s][:, :].unsqueeze(1).broadcast_to([P, RF, K]), ALU.mult)\
                       .then_inc(hG_ready[s], 1)

            def finish(i):
                for s in range(2):
                    dve.wait_ge(o_ps[s], i + 1)
                    dve.wait_ge(xb_ready[s], i + 1)
                    dve.tensor_tensor(fin[s][:, :], CX[s][:, :], xr[s][:, :], ALU.add).then_inc(fin_ready[s], 1)

            maxima(0)
            with dve.Fori(0, NPAIR - 1) as i:
                context_and_gates(i)
                maxima(i + 1)
                finish(i)
            context_and_gates(NPAIR - 1)
            finish(NPAIR - 1)

        @block.tensor
        def _(pe):
            def over_x():
                wait_jobs(pe, NFIRST)
                with pe.Fori(0, NPAIR) as i:
                    for s in range(2):
                        pe.wait_ge(x_in[s], 16 * i + 16)
                        for c in range(C):
                            last = pe.transpose(X[s][:, c * P:(c + 1) * P], xs[s][:, c::C], ident[:, :])
                        last.then_inc(xT_ps, 1)
                    pe.wait_ge(xT_ready, 2 * i + 2)
                    for c in range(C):
                        last = pe.matmul(DN[0][:, 0:2 * P], la_sb[:, c, :], xT[:, c, :, :], start=(c == 0), stop=(c == C - 1))
                    last.then_inc(u_ps, 1)

                    for r in range(REP):
                        o = X[0][:, 2 * r * P:(2 * r + 2) * P]
                        for c in range(C):
                            pe.matmul(o, wf[:, c, r * P:(r + 1) * P], xT[:, c, :, :], start=(c == 0), stop=False)
                        if r == 0:
                            pe.wait_ge(u_ready, i + 1)
                        last = pe.matmul(o, wf[:, C, r * P:(r + 1) * P], uT[:, :, :], start=False, stop=True)
                    last.then_inc(q_ps, 1)
                    for s in range(2):
                        for c in range(C):
                            pe.matmul(CX[s][:, 0:KV], xT[:, c, s, :], wf[:, c, D:D + KV], start=(c == 0), stop=False)
                        last = pe.matmul(CX[s][:, 0:KV], uT[:, s, :], wf[:, C, D:D + KV], start=False, stop=True)
                    last.then_inc(kv_ps, 1)
                    for c in range(C):
                        last = pe.matmul(DN[1][:, 0:2 * P], cbT[:, c, :], xT[:, c, :, :], start=(c == 0), stop=(c == C - 1))
                    last.then_inc(zx_ps, 1)
                    pe.wait_ge(qlow_ready, i + 1)
                pe.wait_ge(kv_ready, NPAIR)
                for g in range(G):
                    last = pe.transpose(X[0][:, g * P:(g + 1) * P], kn[:, g, :, :].rearrange("p j d -> p (j d)"), ident[:, :])
                last.then_inc(kT_ps, 1)
                pe.wait_ge(zx_ready, NPAIR)

            pe.wait_ge(consts, 1)
            pe.wait_ge(w_in, 48)
            for j, job in enumerate(jobs):
                kind, n, part = job
                o = job_bank(j)
                if j == NFIRST:
                    over_x()
                if NFIRST <= j < NFIRST + NB:
                    if j == NFIRST + NB - 2:
                        pe.wait_ge(klow_ready, 1)
                elif j >= NB:
                    pe.wait_ge(pre_out[j % 2], (j - NB) // 2 + 1)
                if kind == "fold":
                    if n == C and part == "q":
                        pe.wait_ge(lora_in, 32 * NBATCH)
                    if n == C + 1 and part == "q":
                        pe.wait_ge(bias_in, 48)
                    rhs = wq_sb if part == "q" else wkv_sb
                    for c in range(C):
                        if n < C:
                            lhsT = w_sb[:, c, n::C]
                        else:
                            lhsT = lb_sb[:, c, :] if n == C else b_sb[:, c:c + 1].broadcast_to([P, P])
                        last = pe.matmul(o[:, 0:rhs.shape[2]], lhsT, rhs[:, c, :], start=(c == 0), stop=(c == C - 1))
                elif kind == "bias_cols":
                    wait_jobs(pe, at[("fold", C + 1, "kv")] + 1)
                    for r in range(REP):
                        last = pe.matmul(o[:, r:r + 1], wf[0:1, C + 1, r * P:(r + 1) * P], ident[0:1, 0:1],
                                         start=True, stop=True)
                elif kind in ("cbT", "woT", "faT", "wrT"):
                    if kind == "cbT":
                        pe.wait_ge(cond2_in, 32 * NBATCH)
                    if kind == "woT" and n == 0:
                        pe.wait_ge(wo_in, 16 * G)
                    if kind == "faT" and n == 0:
                        pe.wait_ge(fa_in, 48)
                    rows = {"cbT": cb_sb[:, :], "woT": wo_sb[:, n % REP, :], "faT": fa_sb[:, n, :], "wrT": wr_sb[:, :]}[kind]
                    m = rows.shape[0]
                    for c in range(C):
                        last = pe.transpose(o[:, c * m:(c + 1) * m], rows[:, c::C], ident[0:m, 0:m])
                elif kind == "wob":
                    wait_jobs(pe, at[("woT", REP - 1)] + 1)
                    for r in range(REP):
                        for c in range(C):
                            last = pe.matmul(o[:, r * P:(r + 1) * P], woT[:, c, r, :], cbT[:, c, :],
                                             start=(c == 0), stop=(c == C - 1))
                elif kind == "bz":
                    wait_jobs(pe, at[("cbT", 0)] + 1)
                    for c in range(C):
                        last = pe.matmul(o[:, 0:1], cbT[:, c, :], bo_sb[:, c:c + 1], start=(c == 0), stop=(c == C - 1))
                else:
                    wait_jobs(pe, at[("wrT", 0)] + 1)
                    lo, hi = 512 * n, min(512 * n + 512, NH + K)
                    for c in range(C):
                        last = pe.matmul(o[:, 0:hi - lo], ca_sb[:, c, :], faT[:, c, lo:hi],
                                         start=(c == 0), stop=(c == C - 1))
                last.then_inc(pre_ps, 1)
            wait_jobs(pe, len(jobs))
            pe.wait_ge(zeroed, 2)

            def experts_out(i, s, n):
                if n == 0:
                    pe.wait_ge(hGT_ready[s], i + 1)
                mmul = pe.matmul(CX[s][:, :], hGT[s][:, n, :], fb_sb[:, n, :], start=False, stop=(n == NI - 1))
                if n == NI - 1:
                    mmul.then_inc(o_ps[s], 1)

            def scores(i, before=None):
                for u in range(REP):
                    for s in range(2):
                        if u == 0:
                            pe.wait_ge(qk_in[s], 6 * 16 * (i + 1))
                            if before is not None:
                                pe.wait_ge(hGT_ready[s], before + 1)
                        else:
                            pe.wait_ge(max_ready[s], 4 * i + u)
                        for half in range(2):
                            pe.matmul(X[s][:, half * 512:(half + 1) * 512], identb[:, :], causal[:, :, :],
                                      start=True, stop=False)
                            for j in (2 * half, 2 * half + 1):
                                last = pe.matmul(X[s][:, j * 2 * P:(j + 1) * 2 * P], QX[s][0:96, j, u * P:(u + 1) * P],
                                                 KX[s][0:96, 2 * j:2 * j + 2, :], start=False, stop=(j % 2 == 1))
                        last.then_inc(s_ps[s], 1)
                        if before is not None:
                            experts_out(before, 0, 2 * u + s)
                for s in range(2):
                    pe.wait_ge(m_ready[s], i + 1)
                    for r in range(REP):
                        last = pe.matmul(DN[s][96:96 + 2 * G, r * P:(r + 1) * P], mhl[s][:, r, :, :], identb[:, :],
                                         start=True, stop=True)
                    last.then_inc(mT_ps[s], 1)
                    if before is not None:
                        experts_out(before, 1, s)
                for u in range(4):
                    for s in range(2):
                        pe.wait_ge(mT_ready[s], 4 * i + u + 1)
                        if u:
                            pe.wait_ge(exp_ready[s], 4 * i + u)
                        for j in range(2):
                            last = pe.matmul(X[s][:, j * 512:(j + 1) * 512], KX[s][:, 2 * u + j, :], QX[s][:, u, :],
                                             start=True, stop=True)
                        last.then_inc(st_ps[s], 1)
                        if before is not None and 2 * u + s < NI - 2:
                            experts_out(before, 1, 2 * u + s + 2)

            def attention_and_hidden(i):
                for s in range(2):
                    pe.wait_ge(pm_ready[s], 4 * i + 4)
                    pe.wait_ge(vpad_ready[s], i + 1)
                    for o, done, v in ((DN[s], den_ps[s], None), (CX[s], pv_ps[s], vpad[s])):
                        for e in range(2):
                            for l in range(4):
                                lhsT = v[:, 2 * l + e, :] if v is not None else onespad[:, e, :]
                                last = pe.matmul(o[32 * l:32 * l + 32, :], lhsT, PT[s][:, 2 * l + e, :],
                                                 start=(e == 0), stop=(e == 1))
                        last.then_inc(done, 1)
                for s in range(2):
                    pe.wait_ge(ctx_ready[s], i + 1)
                    for r in range(REP):
                        last = pe.matmul(DN[s][:, 0:P], wob[:, r, :], ctxT[:, r, s, :], start=(r == 0), stop=(r == REP - 1))
                    last.then_inc(z_ps[s], 1)
                for s in range(2):
                    pe.wait_ge(z_ready[s], i + 1)
                    pe.matmul(DN[s][:, 256:256 + K], zT[s], mm[:, NH:NH + K], start=True, stop=True)\
                      .then_inc(r_ps[s], 1)
                    for half in range(2):
                        last = pe.matmul(X[s][:, half * 512:(half + 1) * 512], zT[s],
                                         mm[:, half * 512:(half + 1) * 512], start=True, stop=True)
                    last.then_inc(h_ps[s], 1)
                for s in range(2):
                    for r in range(REP):
                        pe.matmul(CX[s][:, :], ctxT[:, r, s, :], wo_sb[:, r, :], start=(r == 0), stop=False)
                    pe.wait_ge(hG_ready[s], i + 1)
                    for n in range(NI):
                        last = pe.transpose(X[s][:, n * P:(n + 1) * P], hG[s][:, n * P:(n + 1) * P], ident[:, :])
                    last.then_inc(hGT_ps[s], 1)

            pe.wait_ge(fb_ready, 1)
            scores(0)
            with pe.Fori(0, NPAIR - 1) as i:
                attention_and_hidden(i)
                scores(i + 1, before=i)
                for s in range(2):
                    pe.wait_ge(fin_ready[s], i + 1)
            attention_and_hidden(NPAIR - 1)
            for s in range(2):
                for n in range(NI):
                    experts_out(NPAIR - 1, s, n)


_INS = ['x', 'itok_B_14_62', 'itok_B_3_7', 'L0_cond_W', 'L0_cond_b', 'L0_cond_lora_A', 'L0_cond_lora_B',
        'L0_attn_Wq', 'L0_attn_Wkv', 'L0_attn_Wo', 'L0_attn_bo', 'L0_cond2_A', 'L0_cond2_B',
        'L0_ffn_A', 'L0_ffn_B', 'L0_ffn_Wr']
_OUTS = [((8, 128, 512), 'float32')]


def kernel(**inputs):
    import numpy as _np
    import concourse.bacc as _bacc
    from concourse import mybir as _mybir
    from concourse.bass_utils import run_bass_kernel_spmd as _run

    nc = _bacc.Bacc("TRN2", target_bir_lowering=False, num_devices=1)
    arrays, args = {}, []
    for name in _INS:
        a = _np.ascontiguousarray(inputs[name])
        arrays[f"in_{name}_dram"] = a
        args.append(nc.dram_tensor(f"in_{name}_dram", a.shape, _mybir.dt.from_np(a.dtype), kind="ExternalInput").ap())
    for i, (shape, dtype) in enumerate(_OUTS):
        dt = _mybir.dt.from_np(_np.dtype(dtype))
        args.append(nc.dram_tensor(f"out_{i}_dram", shape, dt, kind="ExternalOutput").ap())
    adaln_attn_ffn_kernel(nc, *args)
    r = _run(nc, [arrays], core_ids=[0])
    return r.results[0]["out_0_dram"]
```

```python
from contextlib import ExitStack

import concourse.bass as bass
from concourse import mybir

F32 = mybir.dt.float32
F32R = mybir.dt.float32r
BF16 = mybir.dt.bfloat16
I32 = mybir.dt.int32
ALU = mybir.AluOpType
ACT = mybir.ActivationFunctionType
AX_X = mybir.AxisListType.X

P = 128


def adaln_attn_ffn_kernel(nc, x, cond_ids, cond2_ids, W, b, lora_A, lora_B, Wq, Wkv, Wo, bo,
                          cond2_A, cond2_B, ffn_A, ffn_B, Wr, out):
    NBATCH, T, D = x.shape
    NPAIR = NBATCH // 2
    R = lora_A.shape[2]
    NLORA, NCOND2 = lora_A.shape[0], cond2_A.shape[0]
    KV = Wkv.shape[1]
    H, G, HD = 32, 8, 16
    REP = H // G
    C = D // P
    K, RF, _ = ffn_A.shape
    NI = K * RF // P
    NH = K * RF
    TOP8 = 2
    SCALE = float(HD) ** -0.5
    LORA_SCALE, FFN_SCALE = 2.0, 2.0
    FAR = -3.0e38
    assert T == P and NBATCH * R == P and G * HD == P and C == REP == 4 and 2 * K == P

    with ExitStack() as ctx:
        def sb(name, shape, dt=F32):
            return ctx.enter_context(nc.sbuf_tensor(name, shape, dt))

        def sem(name):
            return ctx.enter_context(nc.semaphore(name))

        def sems(name):
            return [sem(f"{name}{s}") for s in range(2)]

        ident = sb("ident", [P, P])
        identb = sb("identb", [P, P], BF16)
        causal = sb("causal", [P, 4, P], BF16)
        own = sb("own", [P, NBATCH])
        ownz = sb("ownz", [P, NBATCH])
        own2 = sb("own2", [P, NBATCH])
        maxsel = sb("maxsel", [P, G])
        onespad = sb("onespad", [P, 2, 32])
        fold_parts = sb("fold_parts", [P, 2 * C * (2 * D + KV)], F32R)
        w_parts = fold_parts[:, 0:2 * C * D].rearrange("p (a c n) -> p a c n", a=2, c=C)
        wq_parts = fold_parts[:, 2 * C * D:4 * C * D].rearrange("p (a c n) -> p a c n", a=2, c=C)
        wkv_parts = fold_parts[:, 4 * C * D:].rearrange("p (a c n) -> p a c n", a=2, c=C)
        hGT = fold_parts[:, 0:4 * NH].rearrange("p (a i s t) -> p a i s t", a=2, i=NI, s=2)
        q_parts = fold_parts[:, 0:4 * REP * P].rearrange("p (a s n) -> p a s n", a=2, s=2)
        k_parts = [fold_parts[:, a * G * P:(a + 1) * G * P].rearrange("p (g t) -> p g t", g=G) for a in range(2)]
        xT = [sb("xT", [P, 2, C, 2, P], F32R),
              fold_parts[:, 4 * REP * P:4 * REP * P + 4 * C * P].rearrange("p (a c s t) -> p a c s t", a=2, c=C, s=2)]
        fb_low = fold_parts[:, 4 * NH:4 * NH + NI * D].rearrange("p (i n) -> p i n", i=NI)
        wo_low = fold_parts[:, 4 * NH + NI * D:].rearrange("p (r n) -> p r n", r=REP)
        fb_high = sb("fb_high", [P, NI, D], F32R)
        wo_high = sb("wo_high", [P, REP, D], F32R)
        fb_parts, wo_parts = (fb_high, fb_low), (wo_high, wo_low)
        wf_flat = sb("wf_flat", [P, 2 * (C + 1) * (D + KV)], F32R)
        wf = wf_flat[:, :].rearrange("p (a c n) -> p a c n", a=2, c=C + 1)
        QKN = G // 2 * REP * P
        QX_flat, KX_flat = wf_flat[:, 0:2 * QKN], wf_flat[:, 2 * QKN:2 * QKN + 2 * G * P]
        QX = [QX_flat[:, s * QKN:(s + 1) * QKN].rearrange("p (j n) -> p j n", j=G // 2) for s in range(2)]
        KX = [KX_flat[:, s * G * P:(s + 1) * G * P].rearrange("p (j t) -> p j t", j=G) for s in range(2)]
        ranks_flat = sb("ranks_flat", [P, 3 * 2 * C * P], F32R)
        QUARTER = NBATCH // 2 * R
        adapters = ranks_flat[:, 0:4 * C * P].rearrange("p (a c n) -> p a c n", a=2, c=C)
        la_parts = adapters[:, :, :, QUARTER:3 * QUARTER]
        lb_parts = ranks_flat[:, 4 * C * P:].rearrange("p (a c n) -> p a c n", a=2, c=C)
        mm_parts = ranks_flat[:, 0:2 * (NH + K)].rearrange("p (a n) -> p a n", a=2)
        uT = sb("uT", [P, 2, 2, P], F32R)
        wob_parts = sb("wob_parts", [P, 2, REP, P], F32R)
        b_parts = sb("b_parts", [P, 2, C], F32R)
        big = sb("big", [P, D * RF])
        w_sb = big[:, 0:C * D].rearrange("p (c n) -> p c n", c=C)
        wq_sb = big[:, C * D:2 * C * D].rearrange("p (c n) -> p c n", c=C)
        wkv_sb = big[:, 2 * C * D:2 * C * D + C * KV].rearrange("p (c n) -> p c n", c=C)
        fb_raw = big[:, :]
        faT = big[:, 0:C * (NH + K)].rearrange("p (c n) -> p c n", c=C)
        woT = big[:, C * (NH + K):C * (NH + K) + C * D].rearrange("p (c r n) -> p c r n", c=C, r=REP)
        PT = [big[:, s * G * 4 * P:(s + 1) * G * 4 * P].rearrange("p (g n) -> p g n", g=G) for s in range(2)]
        fa_flat = sb("fa_flat", [P, NI * D])
        fa_sb = fa_flat[:, :].rearrange("p (i n) -> p i n", i=NI)
        hG = [fa_flat[:, n * NH:(n + 1) * NH] for n in range(2)]
        c32, z32 = [[fa_flat[:, at + s * n:at + (s + 1) * n] for s in range(2)]
                    for at, n in ((2 * NH, REP * P), (2 * NH + 2 * REP * P, P))]
        ROUTER = 2 * NH + 2 * (REP + 1) * P
        rs, rest, ex, gate = [[fa_flat[:, at + s * K:at + (s + 1) * K] for s in range(2)]
                              for at in range(ROUTER, ROUTER + 8 * K, 2 * K)]
        gate2 = [sb(f"gate2_{s}", [P, 2 * K]) for s in range(2)]
        wo_sb = sb("wo_sb", [P, REP, D])
        b_sb = sb("b_sb", [P, C])
        bo_sb = sb("bo_sb", [P, C])
        ids = sb("ids", [1, 2, NBATCH], I32)
        ca_sb = sb("ca_sb", [P, C, NBATCH * R])
        cb_sb = sb("cb_sb", [P, D])
        brow = sb("brow", [P, D + KV])
        bq = sb("bq", [P, REP])
        bkv_bc = brow[:, D:D + KV]
        bo_bc = brow[:, 0:D]
        cbT = sb("cbT", [P, C, P])
        bz = sb("bz", [P, 1])
        xs = [sb(f"xs{s}", [P, D]) for s in range(2)]
        xr_flat = sb("xr_flat", [P, 2 * D])
        xr = [xr_flat[:, s * D:(s + 1) * D] for s in range(2)]
        la_sb, lb_sb = [t.rearrange("p (c n) -> p c n", c=C) for t in xr]
        wr_sb = cb_sb[0:K, :]
        kn = xr_flat[:, :].rearrange("p (g j d) -> p g j d", g=G, j=G)
        vn = sb("vn", [P, G, G, HD])
        zx = sb("zx", [P, NBATCH, P])
        vpad = [sb(f"vpad{s}", [P, G, 32]) for s in range(2)]
        q_dram = nc.dram_tensor("q_dram", [2, NBATCH, P, REP * P], F32, kind="Internal").ap()
        k_dram = nc.dram_tensor("k_dram", [2, G, P, P], F32, kind="Internal").ap()
        mx = [sb(f"mx{s}", [P, REP, G]) for s in range(2)]
        mhl = [sb(f"mhl{s}", [P, REP, G, 2], BF16) for s in range(2)]
        rden, ctxT, zT, fin = cb_sb, xT[0], uT, xs
        gateT = cb_sb[:, 0:2 * P]
        top = [sb(f"top{s}", [P, 8 * TOP8]) for s in range(2)]
        nmax = [sb(f"nmax{s}", [P, 1]) for s in range(2)]
        gsum = [sb(f"gsum{s}", [P, 2]) for s in range(2)]

        X = [ctx.enter_context(nc.psum_tensor(f"X{s}", [P, 1024], F32)) for s in range(2)]
        CX = [ctx.enter_context(nc.psum_tensor(f"CX{s}", [P, 512], F32)) for s in range(2)]
        DN = [ctx.enter_context(nc.psum_tensor(f"DN{s}", [P, 512], F32)) for s in range(2)]
        PV = [CX[0][:, :], X[0][:, 0:512]]
        bank = [X[0][:, 0:512], X[0][:, 512:1024], X[1][:, 0:512], X[1][:, 512:1024],
                CX[0][:, :], CX[1][:, :], DN[0][:, :], DN[1][:, :]]
        NB = len(bank)

        consts = sem("consts")
        pool_step = sem("pool_step")
        zeroed = sem("zeroed")
        maxsel_ready, kx_zeroed = sem("maxsel_ready"), sem("kx_zeroed")
        dve_passed, pool_passed = sem("dve_passed"), sem("pool_passed")
        ids_in = sem("ids_in")
        w_in = [sem(f"w_in{c}") for c in range(C)]
        w_high, w_low = sem("w_high"), sem("w_low")
        ranks_high, ranks_low = sem("ranks_high"), sem("ranks_low")
        bias_in, bo_in = sem("bias_in"), sem("bo_in")
        la_in, lb_in, lb_pool_in = sem("la_in"), sem("lb_in"), sem("lb_pool_in")
        ca_in, cb_in = sem("ca_in"), sem("cb_in")
        wo_in = sem("wo_in")
        fa_in = sem("fa_in")
        fb_in = sem("fb_in")
        wr_in = sem("wr_in")
        fb_step = sem("fb_step")
        fb_ready = sem("fb_ready")
        pre_high = sem("pre_high")
        pre_ps = sem("pre_ps")
        pre_out = [sem("pre_dve"), sem("pre_act")]
        x_in = sems("x_in")
        xr_in = sems("xr_in")
        xT_ps, xT_high, xT_ready = sem("xT_ps"), sem("xT_high"), sem("xT_ready")
        u_ps, u_high, u_ready = sem("u_ps"), sem("u_high"), sem("u_ready")
        kv_ps, kv_ready, zx_ready = sem("kv_ps"), sem("kv_ready"), sem("zx_ready")
        kT_ps, khigh_ready, klow_ready, k_stored = sem("kT_ps"), sem("khigh_ready"), sem("klow_ready"), sem("k_stored")
        q_ps, qhigh_ready, qlow_ready, q_stored = sem("q_ps"), sem("qhigh_ready"), sem("qlow_ready"), sem("q_stored")
        qk_in, vpad_ready = sem("qk_in"), sems("vpad_ready")
        s_ps, max_ready, mhi_ready, m_ready = sems("s_ps"), sems("max_ready"), sems("mhi_ready"), sems("m_ready")
        mT_ps, mT_ready = sems("mT_ps"), sems("mT_ready")
        st_ps, exp_ready, pm_ready = sems("st_ps"), sems("exp_ready"), sems("pm_ready")
        den_ps, pv_ps, rden_ready, c_ready, c_high, ctx_ready = (
            sems("den_ps"), sems("pv_ps"), sems("rden_ready"), sems("c_ready"), sems("c_high"), sems("ctx_ready"))
        z_ps, z_sum, z_high, z_ready = sems("z_ps"), sems("z_sum"), sems("z_high"), sems("z_ready")
        r_ps, h_ps = sems("r_ps"), sems("h_ps")
        topk, gexp = sems("topk"), sems("gexp")
        dstep, CHAIN = sems("dstep"), 9
        gT_ps, gT_ready = sem("gT_ps"), sem("gT_ready")
        hG_ready, hGT_high, hGT_ready = sems("hG_ready"), sems("hGT_high"), sems("hGT_ready")
        o_ps, xb_ready, fin_ready, stored = sems("o_ps"), sems("xb_ready"), sems("fin_ready"), sems("stored")

        jobs = [("fold", n, part) for n in range(C + 1) for part in ("q", "kv")]
        jobs += [("bias_row", 0, "q"), ("bias_row", 0, "kv"), ("cbT", 0, ""), ("bias_col", 0, ""), ("bz", 0, "")]
        NFIRST = len(jobs)
        jobs += [("woT", r, "") for r in range(REP)] + [("faT", i, "") for i in range(NI)] + [("wrT", 0, "")]
        NLAST = len(jobs)
        jobs += [("wob", 0, "")] + [("mm", n, "") for n in range(3)]
        NSCORES = len(jobs) - 2
        at = {job: j for j, job in enumerate(jobs)}
        SPLIT = ("fold", "cbT", "wob", "mm")
        by_act = [job[0] not in SPLIT and j % 2 == 1 for j, job in enumerate(jobs)]

        def finished(n):
            return n - sum(by_act[:n]), sum(by_act[:n])

        def wait_jobs(eng, n):
            eng.wait_ge(pre_out[0], finished(n)[0])
            if finished(n)[1]:
                eng.wait_ge(pre_out[1], finished(n)[1])

        def bank_number(j):
            if j < 2 * (C + 1):
                return j % NB
            if j < NFIRST:
                return (j + 2) % NB
            if j < NLAST:
                return (2, 3, 4, 5, 6, 7, 3, 5, 7, 2, 4, 0, 1)[j - NFIRST]
            return 4 + (j - NLAST) % 2

        def job_bank(j):
            return bank[bank_number(j)]

        def wait_bank(eng, j):
            k = max(k for k in range(j) if bank_number(k) == bank_number(j))
            eng.wait_ge(pre_out[by_act[k]], finished(k + 1)[by_act[k]])

        def job_io(job):
            kind, n, part = job
            o = job_bank(at[job])
            if kind == "fold" and part == "q":
                return (o.rearrange("p (g r d) -> p r g d", g=G, r=REP),
                        [wf[:, a, n, 0:D].rearrange("p (r g d) -> p r g d", r=REP, g=G) for a in range(2)])
            if kind == "fold":
                return (o[:, 0:KV].rearrange("p (g t d) -> p t g d", g=G, t=2),
                        [wf[:, a, n, D:D + KV].rearrange("p (t g d) -> p t g d", t=2, g=G) for a in range(2)])
            if kind == "bias_row" and part == "q":
                return (o.rearrange("p (g r d) -> p r g d", g=G, r=REP),
                        brow[:, 0:D].rearrange("p (r g d) -> p r g d", r=REP, g=G))
            if kind == "bias_row":
                return (o[:, 0:KV].rearrange("p (g t d) -> p t g d", g=G, t=2),
                        bkv_bc.rearrange("p (t g d) -> p t g d", t=2, g=G))
            if kind == "bias_col":
                return o[:, 0:REP], bq[:, :]
            if kind == "cbT":
                return (o.rearrange("p (c q n) -> p c q n", c=C, q=2),
                        [adapters[:, a].rearrange("p c (q n) -> p c q n", q=4)[:, :, 0::3, :] for a in range(2)])
            if kind == "woT":
                return o.rearrange("p (c n) -> p c n", c=C), woT[:, :, n, :]
            if kind == "faT":
                return o.rearrange("p (c n) -> p c n", c=C), faT[:, :, n * P:(n + 1) * P]
            if kind == "wrT":
                return o[:, 0:C * K].rearrange("p (c n) -> p c n", c=C), faT[:, :, NH:NH + K]
            if kind == "wob":
                return o.rearrange("p (r n) -> p r n", r=REP), [wob_parts[:, a] for a in range(2)]
            if kind == "bz":
                return o[:, 0:1], bz[:, :]
            lo, hi = 512 * n, min(512 * n + 512, NH + K)
            return o[:, 0:hi - lo], [mm_parts[:, a, lo:hi] for a in range(2)]

        def place(n):
            return (n + NBATCH // 2) % NBATCH

        def load_wqkv(eng, c):
            eng.dma_start(wq_sb[:, c, :], Wq.rearrange("(p c) n -> p c n", c=C)[:, c]).then_inc(w_in[c], 16)
            eng.dma_start(wkv_sb[:, c, :], Wkv.rearrange("(p c) n -> p c n", c=C)[:, c]).then_inc(w_in[c], 16)

        def load_lora_B(eng, first, end, done):
            with eng.Fori(first, end) as n:
                a = eng.value_load(ids[0:1, 0, bass.ds(n, 1)], min_val=0, max_val=NLORA - 1)
                eng.dma_start(lb_sb[:, :, bass.ds(R * n, R)], lora_B[bass.ds(a, 1)].rearrange(
                    "a (p c) r -> p (a c) r", c=C)).then_inc(done, 16)

        block = ctx.enter_context(nc.Block())

        @block.sync
        def _(sp):
            for c in range(2):
                sp.dma_start(w_sb[:, c, :], W.rearrange("(p c) n -> p c n", c=C)[:, c]).then_inc(w_in[c], 16)
                if c:
                    load_wqkv(sp, c)
            sp.dma_start(ids[:, 0, :], cond_ids.rearrange("(a n) -> a n", a=1)).then_inc(ids_in, 16)
            sp.dma_start(ids[:, 1, :], cond2_ids.rearrange("(a n) -> a n", a=1)).then_inc(ids_in, 16)
            for c in range(2, C):
                sp.dma_start(w_sb[:, c, :], W.rearrange("(p c) n -> p c n", c=C)[:, c]).then_inc(w_in[c], 16)
                load_wqkv(sp, c)
            sp.dma_start(b_sb[:, :], b.rearrange("(p c) -> p c", c=C)).then_inc(bias_in, 16)
            sp.dma_start(bo_sb[:, :], bo.rearrange("(p c) -> p c", c=C)).then_inc(bias_in, 16)
            for s in range(2):
                sp.dma_start(xs[s][:, :], x[s]).then_inc(x_in[s], 16)
            sp.wait_ge(ids_in, 32)
            load_lora_B(sp, 0, NBATCH // 2, lb_in)
            for first in (0, NBATCH // 2):
                with sp.Fori(0, NBATCH // 2) as n:
                    a = sp.value_load(ids[0:1, 0, bass.ds(n + first, 1)], min_val=0, max_val=NLORA - 1)
                    sp.dma_start(la_sb[:, :, bass.ds(R * n + R * place(first), R)], lora_A[bass.ds(a, 1)].rearrange(
                        "a (p c) r -> p (a c) r", c=C)).then_inc(la_in, 16)

            def load_x(i):
                sp.wait_ge(xT_ps, 2 * i)
                for s in range(2):
                    sp.dma_start(xs[s][:, :], x[bass.ds(2 * i + s, 1)].rearrange("a t n -> (a t) n")).then_inc(x_in[s], 16)

            fbv = ffn_B.rearrange("k n r -> k (n r)")
            sp.wait_ge(w_low, C)
            sp.dma_start(fb_raw[0:K, :], fbv).then_inc(fb_in, 16)
            sp.dma_start(fb_raw[K:2 * K, 0:D * RF - 1], fbv[:, 1:D * RF]).then_inc(fb_in, 16)
            load_x(1)
            for g in range(G):
                sp.dma_start(wo_sb[HD * g:HD * (g + 1), :, :],
                             Wo.rearrange("(g r d) n -> g d r n", g=G, r=REP)[g]).then_inc(wo_in, 16)
            sp.wait_ge(pre_ps, at[("cbT", 0, "")] + 1)
            sp.dma_start(wr_sb, Wr).then_inc(wr_in, 16)
            sp.sem_inc(q_stored, 16)

            def load_q(i):
                for a, part in enumerate((0, 0, 1)):
                    sp.dma_start(QX_flat[32 * a:32 * a + 32, :].bitcast(F32).rearrange("x (s j f) -> x s j f", s=2, j=G // 2),
                                 q_dram[part, bass.ds(2 * i, 2)].rearrange("s (j x) f -> x s j f", x=32))\
                      .then_inc(qk_in, 16)

            def load_k(i):
                for a, part in enumerate((0, 1, 0)):
                    for e in range(2):
                        rows = KX_flat[32 * a + HD * e:32 * a + HD * (e + 1), :].bitcast(F32)
                        sp.dma_start(rows.rearrange("d (s l e t) -> d s l e t", s=2, e=2, t=P)[:, :, :, e],
                                     k_dram[part, bass.ds(2 * i, 2)].rearrange("s (l e d) t -> e d s l t", e=2, d=HD)[e])\
                          .then_inc(qk_in, 16)

            def store_q(i):
                sp.wait_ge(qlow_ready, i + 1)
                for a in range(2):
                    sp.dma_start(q_dram[a, bass.ds(2 * i, 2)].rearrange("n p f -> p n f"), q_parts[:, a, :, :].bitcast(F32))\
                      .then_inc(q_stored, 16)

            with sp.Fori(0, NPAIR - 2) as i:
                load_x(i + 2)
                store_q(i)
            for c2 in range(2):
                sp.dma_start(fa_sb[K * c2:K * (c2 + 1), :, :],
                             ffn_A.rearrange("k (i c) n -> c k i n", c=2)[c2]).then_inc(fa_in, 16)
            for i in (NPAIR - 2, NPAIR - 1):
                store_q(i)
            for a, signal in enumerate((khigh_ready, klow_ready)):
                sp.wait_ge(signal, 1)
                sp.dma_start(k_dram[a].rearrange("g p t -> p g t"), k_parts[a].bitcast(F32)).then_inc(k_stored, 16)
            sp.wait_ge(kT_ps, 1)
            sp.wait_ge(q_stored, 32 * NPAIR + 16)
            load_q(0)
            sp.wait_ge(k_stored, 32)
            sp.wait_ge(kx_zeroed, 2)
            load_k(0)
            for s in range(2):
                sp.dma_start(xr[s], x[s]).then_inc(xr_in[s], 16)

            def store(i, s):
                sp.wait_ge(fin_ready[s], i + 1)
                sp.dma_start(out[bass.ds(2 * i + s, 1)].rearrange("a t n -> (a t) n"), fin[s][:, :])\
                  .then_inc(stored[s], 16)

            def load_next(i):
                sp.wait_ge(st_ps[1], 4 * i)
                load_q(i)
                load_k(i)

            load_next(1)
            def store_pair(i):
                for s in range(2):
                    store(i, s)
                    sp.dma_start(xr[s], x[bass.ds(2 * i + 2 + s, 1)].rearrange("a t n -> (a t) n"))\
                      .then_inc(xr_in[s], 16)

            with sp.Fori(0, NPAIR - 2) as i:
                load_next(i + 2)
                store_pair(i)
            store_pair(NPAIR - 2)
            for s in range(2):
                store(NPAIR - 1, s)
            for s in range(2):
                sp.wait_ge(stored[s], 16 * NPAIR)

        @block.gpsimd
        def _(pool):
            steps = [0]

            def then_wait(ins):
                steps[0] += 1
                ins.then_inc(pool_step, 1)
                pool.wait_ge(pool_step, steps[0])

            def band(t, low, high, pattern):
                then_wait(pool.memset(t, 1.0))
                then_wait(pool.affine_select(out=t, in_=t, compare_op=ALU.is_ge, fill=0.0, base=-low,
                                             pattern=[[-a, n] for a, n in pattern], channel_multiplier=1))
                then_wait(pool.affine_select(out=t, in_=t, compare_op=ALU.is_ge, fill=0.0, base=high,
                                             pattern=[[a, n] for a, n in pattern], channel_multiplier=-1))

            pool.wait_ge(ids_in, 32)
            load_lora_B(pool, NBATCH // 2, NBATCH, lb_pool_in)
            for n in range(NBATCH):
                a = pool.value_load(ids[0:1, 1, n:n + 1], min_val=0, max_val=NCOND2 - 1)
                pool.dma_start(cb_sb[R * place(n):R * (place(n) + 1), :],
                               cond2_B[bass.ds(a, 1)].rearrange("a r n -> (a r) n")).then_inc(cb_in, 16)
            band(ident[:, :], 0, 0, [(1, P)])
            then_wait(pool.tensor_copy(identb[:, :], ident[:, :]))
            band(own[:, :], 0, R - 1, [(R, NBATCH)])
            for n in (0, NBATCH // 2):
                then_wait(pool.tensor_copy(ownz[:, n:n + NBATCH // 2], own[:, place(n):place(n) + NBATCH // 2]))
            then_wait(pool.tensor_scalar(own2[:, :], own[:, :], LORA_SCALE, None, ALU.mult))
            then_wait(pool.memset(causal[:, :, :], 0.0))
            then_wait(pool.affine_select(out=causal[:, :, :], in_=causal[:, :, :], compare_op=ALU.is_ge,
                                         fill=FAR, base=0, pattern=[[0, 4], [-1, P]], channel_multiplier=1))
            band(maxsel[:, :], 3 * 32, 3 * 32 + 1, [(2, G)])
            pool.memset(onespad[:, :, :], 0.0).then_inc(pool_step, 1)
            pool.wait_ge(pool_step, steps[0] + 1)
            pool.memset(onespad[:, 0, 0:HD], 1.0)
            pool.memset(onespad[:, 1, HD:2 * HD], 1.0).then_inc(consts, 1)
            for first in (0, NBATCH // 2):
                with pool.Fori(0, NBATCH // 2) as n:
                    a = pool.value_load(ids[0:1, 1, bass.ds(n + first, 1)], min_val=0, max_val=NCOND2 - 1)
                    pool.dma_start(ca_sb[:, :, bass.ds(R * n + R * place(first), R)], cond2_A[bass.ds(a, 1)].rearrange(
                        "a (p c) r -> p (a c) r", c=C)).then_inc(ca_in, 16)
            pool.wait_ge(fb_in, 32)
            fbv = fb_raw.rearrange("p (n i c) -> p i n c", i=NI, c=2)[:, :, :, 0]
            for q in range(4):
                pool.tensor_copy(fb_high[:, 2 * q:2 * q + 2, :], fbv[:, 2 * q:2 * q + 2, :]).then_inc(fb_step, 1)
            pool.wait_ge(pre_ps, at[("bias_row", 0, "kv")] + 1)
            for q in range(4):
                pool.wait_ge(fb_step, q + 1)
                last = pool.tensor_tensor(fb_low[:, 2 * q:2 * q + 2, :], fbv[:, 2 * q:2 * q + 2, :],
                                          fb_high[:, 2 * q:2 * q + 2, :].bitcast(F32), ALU.subtract)
            last.then_inc(fb_ready, 1)
            pool.wait_ge(wo_in, 16 * G)
            pool.tensor_copy(wo_high[:, :, :], wo_sb[:, :, :]).then_inc(fb_step, 1)
            pool.wait_ge(fb_step, 5)
            pool.tensor_tensor(wo_low, wo_sb[:, :, :], wo_high[:, :, :].bitcast(F32), ALU.subtract).then_inc(fb_ready, 1)

            def prepare(i):
                for s in range(2):
                    v = vn[:, bass.ds(2 * i + s, 1), :, :].rearrange("p n (l e) d -> p (n l) e d", e=2)
                    o = vpad[s][:, :, :].rearrange("p (l e) d -> p l e d", e=2)
                    pool.tensor_copy(o[:, :, 0, 0:HD], v[:, :, 0, :])
                    pool.tensor_copy(o[:, :, 1, HD:2 * HD], v[:, :, 1, :]).then_inc(vpad_ready[s], 1)

            def masks(i):
                for s in range(2):
                    for u in range(4):
                        pool.wait_ge(exp_ready[s], 4 * i + u + 1)
                        pool.sem_inc(pool_passed, 1)
                        pt = PT[s][:, 2 * u:2 * u + 2, :].rearrange("p g (r q) -> p (g r) q", q=P)
                        pool.affine_select(out=pt, in_=pt, compare_op=ALU.is_ge, fill=0.0, base=0,
                                           pattern=[[0, 2 * REP], [1, P]], channel_multiplier=-1)\
                            .then_inc(pm_ready[s], 1)

            def residual(i):
                for s in range(2):
                    pool.wait_ge(xr_in[s], 16 * i + 16)
                    pool.tensor_tensor(xr[s], xr[s], bo_bc, ALU.add).then_inc(xb_ready[s], 1)

            def context_low(i):
                pool.wait_ge(c_high[0], i + 1)
                pool.tensor_tensor(ctxT[:, 1, :, 0, :], c32[0].rearrange("p (r t) -> p r t", r=REP),
                                   ctxT[:, 0, :, 0, :].bitcast(F32), ALU.subtract).then_inc(ctx_ready[0], 1)

            def hidden_low(i):
                for n in range(2):
                    half = slice(n * NI // 2, (n + 1) * NI // 2)
                    pool.wait_ge(hGT_high[n], i + 1)
                    pool.tensor_tensor(hGT[:, 1, half], hG[n].rearrange("p (i s t) -> p i s t", i=NI // 2, s=2),
                                       hGT[:, 0, half].bitcast(F32), ALU.subtract).then_inc(hGT_ready[n], 1)

            pool.wait_ge(zeroed, 1)
            pool.wait_ge(bo_in, 16)
            pool.wait_ge(kT_ps, 1)
            pool.wait_ge(fb_ready, 2)
            for s in range(2):
                pool.memset(KX[s][0:96].bitcast(F32), 0.0).then_inc(kx_zeroed, 1)
                pool.wait_ge(kx_zeroed, s + 1)
            for s in range(2):
                pool.tensor_copy(KX[s][96:96 + 2 * G], maxsel[96:96 + 2 * G, :].unsqueeze(2).broadcast_to([2 * G, G, P]))\
                    .then_inc(maxsel_ready, 1)
                pool.wait_ge(maxsel_ready, s + 1)
            prepare(0)
            masks(0)
            with pool.Fori(0, NPAIR - 1) as i:
                context_low(i)
                pool.wait_ge(pv_ps[1], i + 1)
                prepare(i + 1)
                hidden_low(i)
                residual(i)
                masks(i + 1)
            context_low(NPAIR - 1)
            hidden_low(NPAIR - 1)
            residual(NPAIR - 1)

        @block.scalar
        def _(act):
            load_wqkv(act, 0)

            for c in range(C):
                act.wait_ge(w_in[c], 48)
                for parts, raw in ((w_parts, w_sb), (wq_parts, wq_sb), (wkv_parts, wkv_sb)):
                    last = act.activation(parts[:, 0, c], raw[:, c], ACT.Copy)
                last.then_inc(w_high, 1)
            act.wait_ge(bias_in, 32)
            act.activation(b_parts[:, 0], b_sb[:, :], ACT.Copy)
            for half in (lb_in, lb_pool_in):
                act.wait_ge(half, 16 * NBATCH // 2)
            act.activation(lb_parts[:, 0], lb_sb, ACT.Copy).then_inc(ranks_high, 1)

            def act_jobs(first, end):
                for j in range(first, end):
                    src, dst = job_io(jobs[j])
                    if jobs[j][0] in SPLIT:
                        act.wait_ge(pre_ps, j + 1)
                        act.activation(dst[0], src, ACT.Copy).then_inc(pre_high, 1)
                    elif by_act[j]:
                        act.wait_ge(pre_ps, j + 1)
                        act.activation(dst, src, ACT.Copy).then_inc(pre_out[1], 1)

            act_jobs(0, 2 * C + 4)
            act.wait_ge(la_in, 16 * NBATCH)
            act.activation(la_parts[:, 0], la_sb, ACT.Copy).then_inc(ranks_high, 1)
            act_jobs(2 * C + 4, NFIRST - 2)
            def x_high(t, h):
                for s in range(2):
                    act.wait_ge(xT_ps, 2 * t + s + 1)
                    act.activation(xT[h][:, 0, :, s, :], X[1][:, s * 512:(s + 1) * 512].rearrange("p (c t) -> p c t", c=C),
                                   ACT.Copy).then_inc(xT_high, 1)

            def q_high(t):
                act.wait_ge(q_ps, t + 1)
                act.wait_ge(q_stored, 32 * t + 16)
                for r in range(REP):
                    act.activation(q_parts[:, 0, :, r * P:(r + 1) * P],
                                   X[0][:, 2 * r * P:2 * (r + 1) * P].rearrange("p (s t) -> p s t", s=2),
                                   ACT.Identity, bias=bq[:, r:r + 1]).then_inc(qhigh_ready, 1)

            x_high(0, 0)
            act_jobs(NFIRST - 2, NFIRST)
            wait_jobs(act, NFIRST)
            act.dma_start(bo_bc, bo.rearrange("(a n) -> a n", a=1).broadcast_to([P, D])).then_inc(bo_in, 16)
            with act.Fori(0, NPAIR // 2 - 1) as i:
                q_high(2 * i)
                x_high(2 * i + 1, 1)
                q_high(2 * i + 1)
                x_high(2 * i + 2, 0)
            q_high(NPAIR - 2)
            x_high(NPAIR - 1, 1)
            q_high(NPAIR - 1)
            act.wait_ge(kT_ps, 1)
            act.wait_ge(q_stored, 32 * NPAIR + 16)
            act.activation(k_parts[0], X[0][:, :].rearrange("p (g t) -> p g t", g=G), ACT.Copy).then_inc(khigh_ready, 1)
            act.wait_ge(fb_ready, 1)
            act_jobs(NFIRST, len(jobs))

            def numerators(i):
                for s in range(2):
                    for u in range(4):
                        act.wait_ge(st_ps[s], 4 * i + u + 1)
                        act.activation(PT[s][:, 2 * u:2 * u + 2, :], X[u % 2][:, :].rearrange(
                            "p (g n) -> p g n", g=2), ACT.Exp, scale=SCALE).then_inc(exp_ready[s], 1)

            def context_high(i):
                for s in range(2):
                    act.wait_ge(c_ready[s], i + 1)
                    act.activation(ctxT[:, 0, :, s, :], c32[s].rearrange("p (r t) -> p r t", r=REP), ACT.Copy)\
                       .then_inc(c_high[s], 1)

            def experts(i):
                for s in range(2):
                    act.wait_ge(topk[s], i + 1)
                    act.activation(ex[s], rs[s], ACT.Exp, bias=nmax[s][:, :]).then_inc(gexp[s], 1)
                for n in range(2):
                    act.wait_ge(hG_ready[n], i + 1)
                    act.activation(hGT[:, 0, n * NI // 2:(n + 1) * NI // 2],
                                   hG[n].rearrange("p (i s t) -> p i s t", i=NI // 2, s=2), ACT.Copy)\
                       .then_inc(hGT_high[n], 1)

            with act.Fori(0, NPAIR) as i:
                numerators(i)
                context_high(i)
                experts(i)

        @block.vector
        def _(dve):
            for s in range(2):
                last = dve.memset(vpad[s][:, :, :], 0.0)
            last.then_inc(zeroed, 1)
            for c in range(C):
                dve.wait_ge(w_high, c + 1)
                for parts, raw in ((w_parts, w_sb), (wq_parts, wq_sb), (wkv_parts, wkv_sb)):
                    last = dve.tensor_tensor(parts[:, 1, c], raw[:, c], parts[:, 0, c].bitcast(F32), ALU.subtract)
                last.then_inc(w_low, 1)
            dve.wait_ge(ranks_high, 1)
            for parts, raw in ((b_parts, b_sb[:, :]), (lb_parts, lb_sb)):
                last = dve.tensor_tensor(parts[:, 1], raw, parts[:, 0].bitcast(F32), ALU.subtract)
            last.then_inc(ranks_low, 1)

            def dve_jobs(first, end):
                for j in range(first, end):
                    src, dst = job_io(jobs[j])
                    if jobs[j][0] in SPLIT:
                        dve.wait_ge(pre_high, sum(job[0] in SPLIT for job in jobs[:j + 1]))
                        if jobs[j][0] == "cbT":
                            dve.tensor_copy(cbT[:, :, :].rearrange("p c (q n) -> p c q n", q=2), src)
                        dve.tensor_tensor(dst[1], src, dst[0].bitcast(F32), ALU.subtract).then_inc(pre_out[0], 1)
                    elif not by_act[j]:
                        dve.wait_ge(pre_ps, j + 1)
                        dve.tensor_copy(dst, src).then_inc(pre_out[0], 1)

            dve_jobs(0, 2 * C + 4)
            dve.wait_ge(ranks_high, 2)
            dve.tensor_tensor(la_parts[:, 1], la_sb, la_parts[:, 0].bitcast(F32), ALU.subtract).then_inc(ranks_low, 1)
            dve_jobs(2 * C + 4, NFIRST - 2)
            dve.wait_ge(consts, 1)

            def x_low(t, h):
                for s in range(2):
                    dve.wait_ge(xT_high, 2 * t + s + 1)
                    dve.tensor_tensor(xT[h][:, 1, :, s, :], X[1][:, s * 512:(s + 1) * 512].rearrange("p (c t) -> p c t", c=C),
                                      xT[h][:, 0, :, s, :].bitcast(F32), ALU.subtract).then_inc(xT_ready, 1)

            def over_x(t, h, more=True):
                dve.wait_ge(u_ps, t + 1)
                for s in range(2):
                    last = dve.tensor_scalar(uT[:, 0, s, :], DN[0][:, s * P:(s + 1) * P],
                                             own2[:, bass.ds(2 * t + s, 1)], None, ALU.mult)
                last.then_inc(u_high, 1)
                dve.wait_ge(u_high, t + 1)
                for s in range(2):
                    last = dve.scalar_tensor_tensor(out=uT[:, 1, s, :], in0=DN[0][:, s * P:(s + 1) * P],
                                                    scalar=own2[:, bass.ds(2 * t + s, 1)],
                                                    in1=uT[:, 0, s, :].bitcast(F32), op0=ALU.mult, op1=ALU.subtract)
                last.then_inc(u_ready, 1)
                for s in range(2):
                    last = dve.tensor_scalar(zx[:, bass.ds(2 * t + s, 1), :].rearrange("p n t -> p (n t)"),
                                             DN[0][:, s * P:(s + 1) * P], bz[:, 0:1],
                                             ownz[:, bass.ds(2 * t + s, 1)], ALU.add, ALU.mult)
                last.then_inc(zx_ready, 1)
                for r in range(REP):
                    dve.wait_ge(qhigh_ready, 4 * t + r - r % 2 + 2)
                    last = dve.scalar_tensor_tensor(
                        out=q_parts[:, 1, :, r * P:(r + 1) * P],
                        in0=X[0][:, 2 * r * P:2 * (r + 1) * P].rearrange("p (s t) -> p s t", s=2),
                        scalar=bq[:, r:r + 1], in1=q_parts[:, 0, :, r * P:(r + 1) * P].bitcast(F32),
                        op0=ALU.add, op1=ALU.subtract)
                last.then_inc(qlow_ready, 1)
                if more:
                    x_low(t + 1, 1 - h)
                dve.wait_ge(kv_ps, t + 1)
                for s in range(2):
                    for n, o in enumerate((kn, vn)):
                        last = dve.tensor_tensor(
                            o[:, :, bass.ds(2 * t + s, 1), :].rearrange("p g j d -> p g (j d)"),
                            CX[s][:, n * P:(n + 1) * P].rearrange("p (g d) -> p g d", g=G),
                            bkv_bc[:, n * P:(n + 1) * P].rearrange("p (g d) -> p g d", g=G), ALU.add)
                last.then_inc(kv_ready, 1)

            x_low(0, 0)
            dve_jobs(NFIRST - 2, NFIRST)
            wait_jobs(dve, NFIRST)
            with dve.Fori(0, NPAIR // 2 - 1) as i:
                for h in range(2):
                    over_x(2 * i + h, h)
            for h in range(2):
                over_x(NPAIR - 2 + h, h, more=(h == 0))
            dve.wait_ge(zx_ready, NPAIR)
            dve.wait_ge(fb_ready, 1)
            dve_jobs(NFIRST, NFIRST + 6)
            dve.wait_ge(khigh_ready, 1)
            dve.tensor_tensor(k_parts[1], X[0][:, :].rearrange("p (g t) -> p g t", g=G), k_parts[0].bitcast(F32),
                              ALU.subtract).then_inc(klow_ready, 1)
            dve_jobs(NFIRST + 6, NSCORES)

            def maxima(i, with_jobs=False):
                for u in range(REP):
                    for s in range(2):
                        dve.wait_ge(s_ps[s], 4 * i + u + 1)
                        dve.reduce_max(mx[s][:, u, :], X[s][:, :].rearrange("p (g k) -> p g k", g=G), AX_X)\
                           .then_inc(max_ready[s], 1)
                for s in range(2):
                    dve.wait_ge(max_ready[s], 4 * i + 4)
                    dve.tensor_scalar(mhl[s][:, :, :, 0], mx[s][:, :, :], -1.0, None, ALU.mult)\
                       .then_inc(mhi_ready[s], 1)
                for s in range(2):
                    dve.wait_ge(mhi_ready[s], i + 1)
                    dve.scalar_tensor_tensor(out=mhl[s][:, :, :, 1], in0=mx[s][:, :, :], scalar=-1.0,
                                             in1=mhl[s][:, :, :, 0], op0=ALU.mult, op1=ALU.subtract)\
                       .then_inc(m_ready[s], 1)
                for s in range(2):
                    for j in range(G // 2):
                        if j == 0:
                            dve.wait_ge(mT_ps[s], i + 1)
                            turned = DN[s][96:96 + 2 * G, :]
                        else:
                            dve.wait_ge(mT_ready[s], 4 * i + 1)
                            turned = QX[s][96:96 + 2 * G, 0, :].bitcast(F32)
                        dve.tensor_copy(QX[s][96:96 + 2 * G, j, :], turned).then_inc(mT_ready[s], 1)
                if with_jobs:
                    dve_jobs(NSCORES, len(jobs))

            def finish(i, s):
                dve.wait_ge(o_ps[s], i + 1)
                dve.wait_ge(xb_ready[s], i + 1)
                dve.tensor_tensor(fin[s][:, :], CX[s][:, :], xr[s], ALU.add).then_inc(fin_ready[s], 1)

            def context_and_gates(i, before=None):
                if before is not None:
                    finish(before, 0)
                for s in range(2):
                    dve.wait_ge(den_ps[s], i + 1)
                    dve.reciprocal(rden[:, :], DN[s][:, :]).then_inc(rden_ready[s], 1)
                    dve.wait_ge(rden_ready[s], i + 1)
                    dve.wait_ge(pv_ps[s], i + 1)
                    dve.tensor_tensor(c32[s], PV[s], rden[:, :], ALU.mult).then_inc(c_ready[s], 1)
                    dve.wait_ge(c_ready[s], i + 1)

                def z_sums(s):
                    dve.wait_ge(z_ps[s], i + 1)
                    dve.scalar_tensor_tensor(out=z32[s], in0=DN[s][:, 0:P],
                                             scalar=ownz[:, bass.ds(2 * i + s, 1)],
                                             in1=zx[:, bass.ds(2 * i + s, 1), :].rearrange("p n t -> p (n t)"),
                                             op0=ALU.mult, op1=ALU.add).then_inc(z_sum[s], 1)

                def z_highs(s):
                    dve.wait_ge(z_sum[s], i + 1)
                    dve.tensor_copy(zT[:, 0, s, :], z32[s]).then_inc(z_high[s], 1)

                def z_lows(s):
                    dve.wait_ge(z_high[s], i + 1)
                    dve.tensor_tensor(zT[:, 1, s, :], z32[s], zT[:, 0, s, :].bitcast(F32), ALU.subtract)\
                       .then_inc(z_ready[s], 1)

                z_sums(0)
                dve.wait_ge(c_high[1], i + 1)
                dve.tensor_tensor(ctxT[:, 1, :, 1, :], c32[1].rearrange("p (r t) -> p r t", r=REP),
                                  ctxT[:, 0, :, 1, :].bitcast(F32), ALU.subtract).then_inc(ctx_ready[1], 1)
                z_highs(0)
                z_lows(0)
                z_sums(1)
                z_highs(1)
                z_lows(1)

                def step(n, run):
                    for s in range(2):
                        if n > 1:
                            dve.wait_ge(dstep[s], CHAIN * i + n - 1)
                            dve.sem_inc(dve_passed, 1)
                        run(s).then_inc(dstep[s], 1)

                for s in range(2):
                    dve.wait_ge(r_ps[s], i + 1)
                step(1, lambda s: dve.tensor_copy(rs[s], DN[s][:, 256:256 + K]))
                step(2, lambda s: dve.max(top[s][:, 0:8], rs[s]))
                for s in range(2):
                    dve.wait_ge(dstep[s], CHAIN * i + 2)
                    dve.tensor_scalar(nmax[s][:, :], top[s][:, 0:1], -1.0, None, ALU.mult).then_inc(topk[s], 1)
                step(3, lambda s: dve.match_replace(rest[s], top[s][:, 0:8], rs[s], FAR))
                step(4, lambda s: dve.max(top[s][:, 8:16], rest[s]))
                step(5, lambda s: dve.match_replace(rest[s], top[s][:, 8:16], rest[s], FAR))
                step(6, lambda s: dve.tensor_tensor(rest[s], rest[s], rs[s], ALU.not_equal))
                for s in range(2):
                    dve.wait_ge(gexp[s], i + 1)
                step(7, lambda s: dve.tensor_tensor_reduce(gate[s], ex[s], rest[s], 1.0, 0.0, ALU.mult,
                                                           ALU.add, gsum[s][:, 0:1]))
                step(8, lambda s: dve.reciprocal(gsum[s][:, 1:2], gsum[s][:, 0:1]))
                step(9, lambda s: dve.tensor_scalar(gate2[s].rearrange("p (a k) -> p a k", a=2),
                                                    gate[s].unsqueeze(1).broadcast_to([P, 2, K]), gsum[s][:, 1:2],
                                                    FFN_SCALE, ALU.mult, ALU.mult))
                if before is not None:
                    finish(before, 1)
                dve.wait_ge(gT_ps, i + 1)
                dve.tensor_copy(gateT, DN[0][:, 0:2 * P]).then_inc(gT_ready, 1)
                dve.wait_ge(gT_ready, i + 1)
                for n in range(2):
                    dve.wait_ge(h_ps[n], i + 1)
                    dve.tensor_tensor(hG[n].rearrange("p (i n) -> p i n", i=NI // 2),
                                      X[n][:, :].rearrange("p (i n) -> p i n", i=NI // 2),
                                      gateT.unsqueeze(1).broadcast_to([P, NI // 2, 2 * P]), ALU.mult)\
                       .then_inc(hG_ready[n], 1)

            maxima(0, with_jobs=True)
            context_and_gates(0)
            with dve.Fori(0, NPAIR - 1) as i:
                maxima(i + 1)
                context_and_gates(i + 1, before=i)
            for s in range(2):
                finish(NPAIR - 1, s)

        @block.tensor
        def _(pe):
            def three(o, stationary, moving, start, stop):
                pe.matmul(o, stationary[0], moving[0], start=start, stop=False)
                pe.matmul(o, stationary[0], moving[1], start=False, stop=False)
                return pe.matmul(o, stationary[1], moving[0], start=False, stop=stop)

            def both(view):
                return [view(0), view(1)]

            def turn_x(t):
                for s in range(2):
                    pe.wait_ge(x_in[s], 16 * t + 16)
                    for c in range(C):
                        last = pe.transpose(X[1][:, (s * C + c) * P:(s * C + c + 1) * P], xs[s][:, c::C], ident[:, :])
                    last.then_inc(xT_ps, 1)

            def over_pair(t, h, columns, more=True):
                pe.wait_ge(xT_ready, 2 * t + 2)
                for c in range(C):
                    last = three(DN[0][:, 0:2 * P], both(lambda a: adapters[:, a, c, columns]), both(lambda a: xT[h][:, a, c]),
                                 start=(c == 0), stop=(c == C - 1))
                last.then_inc(u_ps, 1)
                wait_jobs(pe, NFIRST)
                for r in range(REP):
                    o = X[0][:, 2 * r * P:(2 * r + 2) * P]
                    for c in range(C):
                        three(o, both(lambda a: wf[:, a, c, r * P:(r + 1) * P]), both(lambda a: xT[h][:, a, c]),
                              start=(c == 0), stop=False)
                    if r == 0:
                        pe.wait_ge(u_ready, t + 1)
                    last = three(o, both(lambda a: wf[:, a, C, r * P:(r + 1) * P]), both(lambda a: uT[:, a]),
                                 start=False, stop=True)
                last.then_inc(q_ps, 1)
                if more:
                    turn_x(t + 1)
                for s in range(2):
                    for c in range(C):
                        three(CX[s][:, 0:KV], both(lambda a: xT[h][:, a, c, s, :]), both(lambda a: wf[:, a, c, D:D + KV]),
                              start=(c == 0), stop=False)
                    last = three(CX[s][:, 0:KV], both(lambda a: uT[:, a, s, :]), both(lambda a: wf[:, a, C, D:D + KV]),
                                 start=False, stop=True)
                last.then_inc(kv_ps, 1)

            def over_x():
                pe.wait_ge(ranks_low, 2)
                wait_jobs(pe, NFIRST - 2)
                for h in range(2):
                    over_pair(h, h, slice(P, 2 * P))
                for h in range(2):
                    over_pair(NPAIR // 2 + h, h, slice(0, P), more=(h == 0))
                for j in range(NFIRST, NFIRST + 2):
                    run_job(j)
                pe.wait_ge(kv_ready, NPAIR)
                for g in range(G):
                    last = pe.transpose(X[0][:, g * P:(g + 1) * P], kn[:, g, :, :].rearrange("p j d -> p (j d)"), ident[:, :])
                last.then_inc(kT_ps, 1)
                pe.wait_ge(zx_ready, NPAIR)

            def run_job(j):
                kind, n, part = jobs[j]
                o = job_bank(j)
                if NFIRST <= j < NLAST and bank_number(j) < 2:
                    pe.wait_ge(klow_ready, 1)
                else:
                    wait_bank(pe, j)
                if kind in ("fold", "bias_row"):
                    pe.wait_ge(ranks_low, 1)
                    rhs = wq_parts if part == "q" else wkv_parts
                    for c in range(C):
                        lhsT = both(lambda a: lb_parts[:, a, c] if kind == "fold"
                                    else b_parts[:, a, c:c + 1].broadcast_to([P, P]))
                        last = three(o[:, 0:rhs.shape[3]], lhsT, both(lambda a: rhs[:, a, c]),
                                     start=(c == 0), stop=(c == C - 1))
                elif kind == "bias_col":
                    wait_jobs(pe, at[("bias_row", 0, "q")] + 1)
                    for r in range(REP):
                        last = pe.matmul(o[:, r:r + 1], brow[0:1, r * P:(r + 1) * P], ident[0:1, 0:1],
                                         start=True, stop=True)
                elif kind in ("cbT", "woT", "faT", "wrT"):
                    if kind == "cbT":
                        pe.wait_ge(cb_in, 16 * NBATCH)
                    if kind == "woT" and n == 0:
                        pe.wait_ge(wo_in, 16 * G)
                    if kind == "faT" and n == 0:
                        pe.wait_ge(fa_in, 32)
                    if kind == "wrT":
                        pe.wait_ge(wr_in, 16)
                    rows = {"cbT": cb_sb[:, :], "woT": wo_sb[:, n % REP, :], "faT": fa_sb[:, n, :], "wrT": wr_sb}[kind]
                    m = rows.shape[0]
                    for c in range(C):
                        last = pe.transpose(o[:, c * m:(c + 1) * m], rows[:, c::C], ident[0:m, 0:m])
                elif kind == "wob":
                    wait_jobs(pe, at[("woT", REP - 1, "")] + 1)
                    for r in range(REP):
                        for c in range(C):
                            last = pe.matmul(o[:, r * P:(r + 1) * P], woT[:, c, r, :], cbT[:, c, :],
                                             start=(c == 0), stop=(c == C - 1))
                elif kind == "bz":
                    wait_jobs(pe, at[("cbT", 0, "")] + 1)
                    for c in range(C):
                        last = pe.matmul(o[:, 0:1], cbT[:, c, :], bo_sb[:, c:c + 1], start=(c == 0), stop=(c == C - 1))
                else:
                    wait_jobs(pe, at[("wrT", 0, "")] + 1)
                    pe.wait_ge(ca_in, 16 * NBATCH)
                    lo, hi = 512 * n, min(512 * n + 512, NH + K)
                    for c in range(C):
                        last = pe.matmul(o[:, 0:hi - lo], ca_sb[:, c, :], faT[:, c, lo:hi],
                                         start=(c == 0), stop=(c == C - 1))
                last.then_inc(pre_ps, 1)

            for c in range(C):
                for signal, products in ((w_high, ((0, 0),)), (w_low, ((0, 1), (1, 0)))):
                    pe.wait_ge(signal, c + 1)
                    for j in range(2 * C):
                        _, n, part = jobs[j]
                        rhs = wq_parts if part == "q" else wkv_parts
                        for a, b in products:
                            last = pe.matmul(job_bank(j)[:, 0:rhs.shape[3]], w_parts[:, a, c, n::C], rhs[:, b, c],
                                             start=(c == a == b == 0), stop=(c == C - 1 and a == 1))
                        if c == C - 1 and signal is w_low:
                            last.then_inc(pre_ps, 1)
            for j in range(2 * C, NFIRST):
                if jobs[j][0] == "cbT":
                    pe.wait_ge(consts, 1)
                if j == NFIRST - 2:
                    wait_jobs(pe, 4)
                    turn_x(0)
                run_job(j)
            over_x()
            for j in range(NFIRST + 2, NSCORES):
                run_job(j)
            wait_jobs(pe, NLAST)
            pe.wait_ge(maxsel_ready, 2)

            EXPERTS = [(n, 0, b) for n in range(NI) for b in range(2)] + [(n, 1, 0) for n in range(NI)]

            def experts_out(i, s, first, end):
                for m in range(first, end):
                    n, a, b = EXPERTS[m]
                    if n % (NI // 2) == 0 and s == 0 and b == 0:
                        half = n // (NI // 2)
                        pe.wait_ge((hGT_high, hGT_ready)[a][half], i + 1)
                    last = pe.matmul(CX[s][:, :], hGT[:, a, n, s, :], fb_parts[b][:, n, :],
                                     start=False, stop=(m == len(EXPERTS) - 1))
                    if m == len(EXPERTS) - 1:
                        last.then_inc(o_ps[s], 1)

            def scores(i, before=None):
                for u in range(REP):
                    for s in range(2):
                        if u == 0:
                            pe.wait_ge(qk_in, 9 * 16 * (i + 1))
                            if before is not None:
                                pe.wait_ge(hG_ready[s], before + 1)
                        else:
                            pe.wait_ge(max_ready[s], 4 * i + u)
                        for half in range(2):
                            pe.matmul(X[s][:, half * 512:(half + 1) * 512], identb[:, :], causal[:, :, :],
                                      start=True, stop=False)
                            for j in (2 * half, 2 * half + 1):
                                last = pe.matmul(X[s][:, j * 2 * P:(j + 1) * 2 * P], QX[s][0:96, j, u * P:(u + 1) * P],
                                                 KX[s][0:96, 2 * j:2 * j + 2, :], start=False, stop=(j % 2 == 1))
                        last.then_inc(s_ps[s], 1)
                        if before is not None:
                            experts_out(before, 0, 2 * (2 * u + s), 2 * (2 * u + s) + 2)
                    if before is None and u < 2:
                        run_job(NSCORES + u)
                if before is not None:
                    experts_out(before, 0, 16, 20)
                for s in range(2):
                    pe.wait_ge(m_ready[s], i + 1)
                    for r in range(REP):
                        last = pe.matmul(DN[s][96:96 + 2 * G, r * P:(r + 1) * P], mhl[s][:, r, :, :], identb[:, :],
                                         start=True, stop=True)
                    last.then_inc(mT_ps[s], 1)
                    if before is not None:
                        experts_out(before, 0, 20 + 2 * s, 22 + 2 * s)

            def attention_and_hidden(i, before=None):
                def second_scores(s, u):
                    pe.wait_ge(mT_ready[s], 4 * i + u + 1)
                    if u >= 2:
                        pe.wait_ge(exp_ready[s], 4 * i + u - 1)
                    elif s == 1:
                        pe.wait_ge(exp_ready[0], 4 * i + u + 3)
                    for j in range(2):
                        last = pe.matmul(X[u % 2][:, j * 512:(j + 1) * 512], KX[s][0:112, 2 * u + j, :],
                                         QX[s][0:112, u, :], start=True, stop=True)
                    last.then_inc(st_ps[s], 1)

                def fill(first, end):
                    if before is not None:
                        experts_out(before, 1, first, end)

                def denominators(s, e):
                    pe.wait_ge(pm_ready[s], 4 * i + 4)
                    for l in range(4):
                        last = pe.matmul(DN[s][32 * l:32 * l + 32, :], onespad[:, e, :], PT[s][:, 2 * l + e, :],
                                         start=(e == 0), stop=(e == 1))
                    if e == 1:
                        last.then_inc(den_ps[s], 1)

                def contexts(s):
                    pe.wait_ge(vpad_ready[s], i + 1)
                    if before is not None and s == 0:
                        pe.wait_ge(fin_ready[0], before + 1)
                    for e in range(2):
                        for l in range(4):
                            last = pe.matmul(PV[s][32 * l:32 * l + 32, :], vpad[s][:, 2 * l + e, :], PT[s][:, 2 * l + e, :],
                                             start=(e == 0), stop=(e == 1))
                    last.then_inc(pv_ps[s], 1)

                def z_from_context(s, low):
                    for r in range(REP):
                        for b in range(1 if low else 2):
                            last = pe.matmul(DN[s][:, 0:P], wob_parts[:, b, r], ctxT[:, low, r, s, :],
                                             start=(low == r == b == 0), stop=(low == 1 and r == REP - 1))
                    if low:
                        last.then_inc(z_ps[s], 1)

                def attention_out(s, low):
                    for r in range(REP):
                        for b in range(1 if low else 2):
                            pe.matmul(CX[s][:, :], ctxT[:, low, r, s, :], wo_parts[b][:, r, :],
                                      start=(low == r == b == 0), stop=False)

                def router_scores(s):
                    pe.wait_ge(z_ready[s], i + 1)
                    three(DN[s][:, 256:256 + K], both(lambda a: zT[:, a, s, :]),
                          both(lambda a: mm_parts[:, a, NH:NH + K]), start=True, stop=True).then_inc(r_ps[s], 1)

                second_scores(0, 0)
                second_scores(0, 1)
                fill(0, 4)
                second_scores(0, 2)
                fill(4, 6)
                second_scores(0, 3)
                fill(6, 7)
                second_scores(1, 0)
                fill(7, 10)
                second_scores(1, 1)
                fill(10, 11)
                second_scores(1, 2)
                denominators(0, 0)
                second_scores(1, 3)
                denominators(0, 1)
                if before is None:
                    wait_jobs(pe, len(jobs))
                contexts(0)
                for e in range(2):
                    denominators(1, e)
                contexts(1)
                if before is None:
                    pe.wait_ge(fb_ready, 2)
                pe.wait_ge(c_high[0], i + 1)
                z_from_context(0, 0)
                attention_out(0, 0)
                pe.wait_ge(ctx_ready[0], i + 1)
                z_from_context(0, 1)
                attention_out(0, 1)
                pe.wait_ge(c_high[1], i + 1)
                z_from_context(1, 0)
                pe.wait_ge(ctx_ready[1], i + 1)
                z_from_context(1, 1)
                router_scores(0)
                fill(11, 16)
                router_scores(1)
                fill(16, 24)
                for n in range(NI):
                    half, at_n = divmod(n, NI // 2)
                    last = three(X[half][:, at_n * 2 * P:(at_n + 1) * 2 * P], both(lambda a: mm_parts[:, a, n * P:(n + 1) * P]),
                                 both(lambda a: zT[:, a]), start=True, stop=True)
                    if at_n == NI // 2 - 1:
                        last.then_inc(h_ps[half], 1)
                for s in range(2):
                    pe.wait_ge(dstep[s], CHAIN * (i + 1))
                    last = pe.transpose(DN[0][:, s * P:(s + 1) * P], gate2[s][:, :], ident[:, :])
                last.then_inc(gT_ps, 1)
                if before is not None:
                    pe.wait_ge(fin_ready[1], before + 1)
                attention_out(1, 0)
                attention_out(1, 1)

            scores(0)
            attention_and_hidden(0)
            with pe.Fori(0, NPAIR - 1) as i:
                scores(i + 1, before=i)
                attention_and_hidden(i + 1, before=i)
            for s in range(2):
                experts_out(NPAIR - 1, s, 0, len(EXPERTS))


_INS = ['x', 'itok_B_14_62', 'itok_B_3_7', 'L0_cond_W', 'L0_cond_b', 'L0_cond_lora_A', 'L0_cond_lora_B',
        'L0_attn_Wq', 'L0_attn_Wkv', 'L0_attn_Wo', 'L0_attn_bo', 'L0_cond2_A', 'L0_cond2_B',
        'L0_ffn_A', 'L0_ffn_B', 'L0_ffn_Wr']
_OUTS = [((8, 128, 512), 'float32')]


def kernel(**inputs):
    import numpy as _np
    import concourse.bacc as _bacc
    from concourse import mybir as _mybir
    from concourse.bass_utils import run_bass_kernel_spmd as _run

    nc = _bacc.Bacc("TRN2", target_bir_lowering=False, num_devices=1)
    arrays, args = {}, []
    for name in _INS:
        a = _np.ascontiguousarray(inputs[name])
        arrays[f"in_{name}_dram"] = a
        args.append(nc.dram_tensor(f"in_{name}_dram", a.shape, _mybir.dt.from_np(a.dtype), kind="ExternalInput").ap())
    for i, (shape, dtype) in enumerate(_OUTS):
        dt = _mybir.dt.from_np(_np.dtype(dtype))
        args.append(nc.dram_tensor(f"out_{i}_dram", shape, dt, kind="ExternalOutput").ap())
    adaln_attn_ffn_kernel(nc, *args)
    r = _run(nc, [arrays], core_ids=[0])
    return r.results[0]["out_0_dram"]
```
